# Optimizing a Trainium2 kernel written in Bass

```python
import numpy as np
import jax
import jax.numpy as jnp

def _softmax(x, axis=-1):
    return jax.nn.softmax(x, axis=axis)

def _gelu(x):
    return jax.nn.gelu(x, approximate=True)

def _silu(x):
    return jax.nn.silu(x)

def _sigmoid(x):
    return jax.nn.sigmoid(x)

def _layernorm(x, axis=-1, eps=1e-05):
    m = jnp.mean(x, axis=axis, keepdims=True)
    v = jnp.var(x, axis=axis, keepdims=True)
    return (x - m) / jnp.sqrt(v + eps)

def _scatter_add(tgt, idx, src, axis=0):
    return tgt.at[idx].add(src)

def _segment_sum(src, seg, n):
    return jax.ops.segment_sum(src, seg, n)
kernel_name = 'mk_gnn_ffn_d1_gnn_r8_bb52a4'

def setup_inputs(seed: int=0):
    np.random.seed(seed)
    _w = jnp.asarray

    def _rec_inputs():
        import jax
        import jax.numpy as jnp
        _gk = jax.random.key(seed)
        x = -0.0003713 + 1 * jax.random.normal(jax.random.fold_in(_gk, 1), (12500, 256), jnp.float32)
        src = jax.random.randint(jax.random.fold_in(_gk, 2), (200000,), 0, 12500, jnp.int32)
        dst = jnp.minimum((12500 * jax.random.uniform(jax.random.fold_in(_gk, 3), (200000,)) ** 2.0).astype(jnp.int32), 99999)
        _o = jnp.argsort(dst, stable=True)
        src = src[_o]
        dst = dst[_o]
        return (x, src, dst)
    x, src, dst = _rec_inputs()

    def _L0_gnn_setup():
        import jax, jax.numpy as jnp
        import numpy as np
        BN_EPS = 1e-05
        CHANNELS = [256, 512, 1024, 512, 256]

        def _bn(h, gamma, beta):
            m = h.mean(axis=0)
            v = h.var(axis=0)
            return gamma * (h - m) * jax.lax.rsqrt(v + BN_EPS) + beta
        key = jax.random.key(seed)
        N, E = (6250, 100000)
        ks = jax.random.split(key, 16)
        inp = {'x': jax.random.normal(ks[0], (N, CHANNELS[0]), dtype=jnp.float32), 'edge_index': jax.random.randint(ks[1], (2, E), 0, N, dtype=jnp.int32), 'eps': jnp.float32(0.1)}
        for i in range(4):
            cin, cout = (CHANNELS[i], CHANNELS[i + 1])
            inp[f'W{i + 1}'] = jax.random.normal(ks[2 + 3 * i], (cin, cout), dtype=jnp.float32) * (1.0 / np.sqrt(cin))
            inp[f'b{i + 1}'] = jnp.zeros((cout,), dtype=jnp.float32)
            if i < 3:
                inp[f'g{i + 1}'] = jnp.ones((cout,), dtype=jnp.float32)
                inp[f'beta{i + 1}'] = jnp.zeros((cout,), dtype=jnp.float32)
        return inp
    _L0_gnn_all = _L0_gnn_setup()
    _L0_gnn_in = {k: v for k, v in _L0_gnn_all.items() if k in ('eps', 'W1', 'b1', 'g1', 'beta1', 'W2', 'b2', 'g2', 'beta2', 'W3', 'b3', 'g3', 'beta3', 'W4', 'b4')}
    del _L0_gnn_all

    def _L0_ffn_setup():
        import math
        import jax, jax.numpy as jnp
        import numpy as np
        CAPACITY_FACTOR = 1.25
        key = jax.random.key(seed)
        ks = jax.random.split(key, 5)
        B, L, D, F, E = (8, 1024, 256, 1024, 8)
        h = jax.random.normal(ks[0], (B, L, D), dtype=jnp.float32)
        gate_w = jax.random.normal(ks[1], (D, E), dtype=jnp.float32) * 0.02
        gate_b = jnp.zeros((E,), dtype=jnp.float32)
        w1 = jax.random.normal(ks[2], (E, D, F), dtype=jnp.float32) * (1.0 / math.sqrt(D))
        b1 = jnp.zeros((E, F), dtype=jnp.float32)
        w2 = jax.random.normal(ks[3], (E, F, D), dtype=jnp.float32) * (1.0 / math.sqrt(F))
        b2 = jnp.zeros((E, D), dtype=jnp.float32)
        return {'h': h, 'gate_w': gate_w, 'gate_b': gate_b, 'w1': w1, 'b1': b1, 'w2': w2, 'b2': b2}
    _L0_ffn_all = _L0_ffn_setup()
    _L0_ffn_in = {k: v for k, v in _L0_ffn_all.items() if k in ('gate_w', 'gate_b', 'w1', 'b1', 'w2', 'b2')}
    del _L0_ffn_all
    return {'x': x, 'src': src, 'dst': dst, 'L0_gnn_eps': _L0_gnn_in['eps'], 'L0_gnn_W1': _L0_gnn_in['W1'], 'L0_gnn_b1': _L0_gnn_in['b1'], 'L0_gnn_g1': _L0_gnn_in['g1'], 'L0_gnn_beta1': _L0_gnn_in['beta1'], 'L0_gnn_W2': _L0_gnn_in['W2'], 'L0_gnn_b2': _L0_gnn_in['b2'], 'L0_gnn_g2': _L0_gnn_in['g2'], 'L0_gnn_beta2': _L0_gnn_in['beta2'], 'L0_gnn_W3': _L0_gnn_in['W3'], 'L0_gnn_b3': _L0_gnn_in['b3'], 'L0_gnn_g3': _L0_gnn_in['g3'], 'L0_gnn_beta3': _L0_gnn_in['beta3'], 'L0_gnn_W4': _L0_gnn_in['W4'], 'L0_gnn_b4': _L0_gnn_in['b4'], 'L0_ffn_gate_w': _L0_ffn_in['gate_w'], 'L0_ffn_gate_b': _L0_ffn_in['gate_b'], 'L0_ffn_w1': _L0_ffn_in['w1'], 'L0_ffn_b1': _L0_ffn_in['b1'], 'L0_ffn_w2': _L0_ffn_in['w2'], 'L0_ffn_b2': _L0_ffn_in['b2']}

def reference(x, src, dst, L0_gnn_eps, L0_gnn_W1, L0_gnn_b1, L0_gnn_g1, L0_gnn_beta1, L0_gnn_W2, L0_gnn_b2, L0_gnn_g2, L0_gnn_beta2, L0_gnn_W3, L0_gnn_b3, L0_gnn_g3, L0_gnn_beta3, L0_gnn_W4, L0_gnn_b4, L0_ffn_gate_w, L0_ffn_gate_b, L0_ffn_w1, L0_ffn_b1, L0_ffn_w2, L0_ffn_b2):
    import jax
    import jax.numpy as jnp

    def _L0_gnn_ref(x, edge_index, eps, W1, b1, g1, beta1, W2, b2, g2, beta2, W3, b3, g3, beta3, W4, b4):
        import jax, jax.numpy as jnp
        import numpy as np
        BN_EPS = 1e-05
        CHANNELS = [256, 512, 1024, 512, 256]

        def _bn(h, gamma, beta):
            m = h.mean(axis=0)
            v = h.var(axis=0)
            return gamma * (h - m) * jax.lax.rsqrt(v + BN_EPS) + beta
        src, dst = (edge_index[0], edge_index[1])
        agg = jax.ops.segment_sum(x[src], dst, num_segments=x.shape[0])
        h = (1.0 + eps) * x + agg
        h = jax.nn.elu(_bn(h @ W1 + b1, g1, beta1))
        h = jax.nn.elu(_bn(h @ W2 + b2, g2, beta2))
        h = jax.nn.elu(_bn(h @ W3 + b3, g3, beta3))
        return h @ W4 + b4

    def _L0_ffn_ref(h, gate_w, gate_b, w1, b1, w2, b2):
        import math
        import jax, jax.numpy as jnp
        import numpy as np
        CAPACITY_FACTOR = 1.25
        B, L, D = h.shape
        E = gate_w.shape[1]
        T = B * L
        C = max(1, math.ceil(CAPACITY_FACTOR * T / E))
        x = h.reshape(T, D)
        logits = x @ gate_w + gate_b
        probs = jax.nn.softmax(logits, axis=-1)
        idx = jnp.argmax(probs, axis=-1)
        prb = jnp.take_along_axis(probs, idx[:, None], axis=1)[:, 0]
        one_hot = jax.nn.one_hot(idx, E, dtype=jnp.float32)
        pos = (jnp.cumsum(one_hot, axis=0) * one_hot).sum(-1).astype(jnp.int32) - 1
        kept = pos < C
        pos_safe = jnp.where(kept, pos, C)
        buf = jnp.zeros((E, C, D), dtype=h.dtype).at[idx, pos_safe].set(x, mode='drop')
        hmid = jax.nn.relu(jnp.einsum('ecd,edf->ecf', buf, w1) + b1[:, None, :])
        ybuf = jnp.einsum('ecf,efd->ecd', hmid, w2) + b2[:, None, :]
        pos_g = jnp.minimum(pos, C - 1)
        y_tok = ybuf[idx, pos_g] * (prb * kept)[:, None]
        y = y_tok.reshape(B, L, D)
        y = jnp.nan_to_num(y, nan=0.0, posinf=10000.0, neginf=-10000.0)
        return y
    edge_index = jnp.stack([src, dst])
    x = x + _L0_gnn_ref(_layernorm(x, axis=-1), edge_index, L0_gnn_eps, L0_gnn_W1, L0_gnn_b1, L0_gnn_g1, L0_gnn_beta1, L0_gnn_W2, L0_gnn_b2, L0_gnn_g2, L0_gnn_beta2, L0_gnn_W3, L0_gnn_b3, L0_gnn_g3, L0_gnn_beta3, L0_gnn_W4, L0_gnn_b4)
    x = x + _L0_ffn_ref(_layernorm(x, axis=-1)[None], L0_ffn_gate_w, L0_ffn_gate_b, L0_ffn_w1, L0_ffn_b1, L0_ffn_w2, L0_ffn_b2)[0]
    return x

_drawn_inputs = setup_inputs


def setup_inputs(seed=0):
    import zlib

    import numpy as np

    out = dict(_drawn_inputs(seed))
    spreads = {'L0_gnn_b1': (0.0, 0.8),
     'L0_gnn_g1': (1.0, 0.2),
     'L0_gnn_beta1': (0.0, 0.1),
     'L0_gnn_b2': (0.0, 0.8),
     'L0_gnn_g2': (1.0, 0.2),
     'L0_gnn_beta2': (0.0, 0.275),
     'L0_gnn_b3': (0.0, 0.8),
     'L0_gnn_g3': (1.0, 0.2),
     'L0_gnn_beta3': (0.0, 0.1),
     'L0_gnn_b4': (0.0, 0.1),
     'L0_ffn_gate_b': (0.0, 0.1),
     'L0_ffn_b1': (0.0, 0.787),
     'L0_ffn_b2': (0.0, 0.557)}
    factors = {}
    for name, (base, spread) in spreads.items():
        noise = np.random.default_rng([zlib.crc32(name.encode()), seed]).standard_normal(out[name].shape)
        drawn = base * np.exp(spread * noise) if base else spread * noise
        out[name] = jnp.asarray(drawn.astype(out[name].dtype))
    for name, factor in factors.items():
        out[name] = (out[name] * factor).astype(out[name].dtype)
    return out
```

```python
import concourse.bass as bass
from concourse import mybir
from contextlib import ExitStack

F32 = mybir.dt.float32
F32R = mybir.dt.float32r
I32 = mybir.dt.int32
I16 = mybir.dt.int16
ALU = mybir.AluOpType
ACT = mybir.ActivationFunctionType
AX = mybir.AxisListType

P = 128
N, D = 12500, 256
E = 200000
CH = [256, 512, 1024, 512, 256]
LN_EPS = BN_EPS = 1e-5

GROUP = 4 * P
NG = -(-N // GROUP)
NTILES = -(-N // P)
NPAD = NTILES * P
TILE = 500
NT = N // TILE
assert NT == NG and NT % 2 == 1 and NT * TILE == N
LAST = NT - 1
TAIL = N - LAST * GROUP

CPB = 4
EB = CPB * P
BODY = 8
SLOTS = 4
NBLK = -(-E // (EB * BODY)) * BODY
BQ = 4
BP = NBLK // BQ
assert BP * BQ == NBLK and BP <= P

NE, F = 8, 1024
CAP = -(-(5 * N) // (4 * NE))
XT = [GROUP, GROUP, GROUP, CAP - 3 * GROUP]
BUFROWS = -(-(NE * CAP + GROUP) // P) * P
FAR = 1 << 20

VECS = [("L0_gnn_b1", 4), ("L0_gnn_g1", 4), ("L0_gnn_beta1", 4),
        ("L0_gnn_b2", 8), ("L0_gnn_g2", 8), ("L0_gnn_beta2", 8),
        ("L0_gnn_b3", 4), ("L0_gnn_g3", 4), ("L0_gnn_beta3", 4)]
VCOL, _at = {}, 0
for _n, _c in VECS:
    VCOL[_n] = _at
    _at += _c
NVEC = _at
NB1 = NE * F // P


def row_parts(n):
    if not is_last(n):
        return [(0, 4, P)]
    full, rest = divmod(TAIL, P)
    return [(0, full, P), (full, 1, rest)]


def row_tiles(n):
    return [(s, rows) for a, c, rows in row_parts(n) for s in range(a, a + c)]


def static(n):
    return isinstance(n, int)


def is_last(n):
    return static(n) and n == LAST


def over_steps(eng, step):
    step(0, 0)
    step(1, 1)
    with eng.Fori(1, NT // 2) as i:
        step(i * 2, 0)
        step(i * 2 + 1, 1)
    step(LAST, LAST % 2)


def uses(n, par):
    return n // 2 + 1 if static(n) else (n - par) // 2 + 1


def after(eng, sem, value, held):
    eng.wait_ge(sem, value)
    eng.sem_inc(held, 1)


def gnn_ffn_program(nc, a, out):
    def dram(name, shape, dt=F32):
        return nc.dram_tensor(name, shape, dt, kind="Internal").ap()

    xln_d = dram("xln_d", [N, D])
    range_d = dram("range_d", [NBLK, 2], I32)
    h_d = [dram(f"h{k}_d", [CH[k], N]) for k in (1, 2, 3)]
    x1_d = dram("x1_d", [N, D])
    buf_d = dram("buf_d", [BUFROWS, D])
    y_d = dram("y_d", [NE * CAP, D])

    whole = ExitStack()
    with whole:
        def outer(name, shape, dt=F32, scope=whole):
            return scope.enter_context(nc.sbuf_tensor(name, shape, dt))

        ident = outer("ident", [P, P])
        vec = outer("vec", [P, NVEC])
        b1e = outer("b1e", [P, NB1])
        epsln = outer("epsln", [P, 1])
        stats = outer("stats", [P, 8, NT, 6])

        mid = ExitStack()
        with mid:
            w2h = outer("w2h", [P, 4, CH[2]], F32R, mid)
            w2l = outer("w2l", [P, 4, CH[2]], F32R, mid)
            first = ExitStack()
            with first:
                acc = outer("acc", [P, 2, NPAD], F32, first)
                w1h = outer("w1h", [P, 2, CH[1]], F32R, first)
                w1l = outer("w1l", [P, 2, CH[1]], F32R, first)
                edges = ExitStack()
                with edges:
                    src_t = outer("src_t", [P, NBLK * CPB], I32, edges)
                    ndst_t = outer("ndst_t", [P, NBLK * CPB], F32, edges)
                    trow = outer("trow", [1, NBLK * 2], I32, edges)
                    prepare(nc, a, xln_d, range_d, ident, vec, b1e, epsln, w1h, w1l,
                            acc, src_t, ndst_t, trow)
                    aggregate(nc, xln_d, buf_d, acc, src_t, ndst_t, trow)
                layer(nc, 1, a, None, h_d[0], acc, stats, vec, epsln, (w1h, w1l),
                      None, (a["L0_gnn_W2"], w2h, w2l))
            w3raw = outer("w3raw", [P, 8, CH[3]], F32, mid)
            layer(nc, 2, a, h_d[0], h_d[1], None, stats, vec, epsln, (w2h, w2l),
                  None, (a["L0_gnn_W3"], w3raw, None))
            layer(nc, 3, a, h_d[1], h_d[2], None, stats, vec, epsln, (w2h, w2l), w3raw, None)
        gidx = outer("gidx", [P, 4 * NG], I32)
        gate = outer("gate", [P, 4 * NG])
        last_layer(nc, a, h_d[2], x1_d, buf_d, stats, vec, epsln, ident, gidx, gate)
        experts(nc, a, buf_d, y_d, ident, b1e)
        combine(nc, x1_d, y_d, gidx, gate, out)


def prepare(nc, a, xln_d, range_d, ident, vec, b1e, epsln, w1h, w1l,
            acc, src_t, ndst_t, trow):
    ctx = ExitStack()
    with ctx:
        def sb(name, shape, dt=F32):
            return ctx.enter_context(nc.sbuf_tensor("a_" + name, shape, dt))

        sems = []

        def sem(name):
            sems.append(nc.alloc_semaphore("a_" + name))
            return sems[-1]

        src_raw = sb("src_raw", [BP, BQ, EB], I32)
        dst_raw = sb("dst_raw", [BP, BQ, EB], I32)
        src_f, dst_f = src_raw[:, :, :].bitcast(F32), dst_raw[:, :, :].bitcast(F32)
        reach_f = sb("reach_f", [BP, BQ, 2])
        reach = sb("reach", [BP, BQ, 2], I32)
        vraw = sb("vraw", [NVEC, P])
        b1raw = sb("b1raw", [NB1, P])
        ope = sb("ope", [P, 1])
        w1raw = sb("w1raw", [P, 2, CH[1]])
        xg = [sb(f"xg{k}", [P, 4, D]) for k in range(2)]
        xn = [sb(f"xn{k}", [P, 4, D]) for k in range(2)]
        st = [sb(f"st{k}", [P, 4, 6]) for k in range(2)]
        mv = [sb(f"mv{k}", [P, 4, 2]) for k in range(2)]
        rs = [sb(f"rs{k}", [P, 4]) for k in range(2)]
        ps_x = [ctx.enter_context(nc.psum_tensor(f"a_ps_x{k}", [P, 2, GROUP], F32)) for k in range(2)]
        ps_e = [ctx.enter_context(nc.psum_tensor(f"a_ps_e{k}", [P, 512], F32)) for k in range(4)]

        pads, const, held = sem("pads"), sem("const"), sem("held")
        edges_in, vec_in, eps_in, w_in = sem("edges_in"), sem("vec_in"), sem("eps_in"), sem("w_in")
        x_in = [sem(f"x_in{k}") for k in range(2)]
        cast, reached, shifted, range_out, range_in = (sem("cast"), sem("reached"), sem("shifted"),
                                                       sem("range_out"), sem("range_in"))
        src_turned, dst_turned, src_kept, dst_kept = (sem("src_turned"), sem("dst_turned"),
                                                      sem("src_kept"), sem("dst_kept"))
        vec_turned, vec_kept, scaled = sem("vec_turned"), sem("vec_kept"), sem("scaled")
        w_high, w_low = sem("w_high"), sem("w_low")
        summed, moments, rooted, inverse, normed = (sem("summed"), sem("moments"), sem("rooted"),
                                                    sem("inverse"), sem("normed"))
        turned, kept = sem("turned"), sem("kept")
        xln_out = [sem(f"xln_out{k}") for k in range(2)]
        EDGE_LOADS = 6

        ctx.callback(nc.all_engine_barrier)
        ctx.callback(nc.clear_and_free_semaphores, sems)
        xfull = a["x"][0:LAST * GROUP, :].rearrange("(g s p) f -> g p s f", s=4, p=P)
        nfull = xln_d[0:LAST * GROUP, :].rearrange("(g s p) f -> g p s f", s=4, p=P)

        def group(view, n):
            if static(n):
                return view[n]
            return view[bass.ds(n, 1)].rearrange("o p s f -> (o p) s f")

        block = ctx.enter_context(nc.Block())

        @block.sync
        def _(sp):
            def load(n, par):
                if not is_last(n):
                    if not static(n):
                        sp.wait_ge(normed, n - 1)
                    sp.dma_start(xg[par][:, :, :], group(xfull, n)).then_inc(x_in[par], 16)
                else:
                    sp.wait_ge(normed, n - 1)
                    for s, rows in row_tiles(n):
                        at = n * GROUP + s * P
                        sp.dma_start(xg[par][0:rows, s, :], a["x"][at:at + rows, :]).then_inc(x_in[par], 16)

            sp.wait_ge(pads, 2)
            whole_blocks, rest = divmod(E, EB)
            low = (BQ - 1) * BP
            for raw, name in ((src_raw, "src"), (dst_raw, "dst")):
                sp.dma_start(raw[:, 0:BQ - 1, :],
                             a[name][0:low * EB].rearrange("(q p e) -> p q e", q=BQ - 1, e=EB)).then_inc(edges_in, 16)
                sp.dma_start(raw[0:whole_blocks - low, BQ - 1, :],
                             a[name][low * EB:whole_blocks * EB].rearrange("(p e) -> p e", e=EB)).then_inc(edges_in, 16)
                sp.dma_start(raw[whole_blocks - low:whole_blocks - low + 1, BQ - 1, 0:rest],
                             a[name][whole_blocks * EB:E].rearrange("(p e) -> p e", p=1)).then_inc(edges_in, 16)
            over_steps(sp, load)
            sp.wait_ge(shifted, 4)
            sp.dma_start(range_d.rearrange("(q p) c -> p q c", q=BQ), reach[:, :, :]).then_inc(range_out, 16)
            sp.wait_ge(range_out, 16)
            sp.dma_start(trow[:, :], range_d.rearrange("(o b) c -> o (b c)", o=1)).then_inc(range_in, 16)
            sp.wait_ge(range_in, 16)

        @block.gpsimd
        def _(pool):
            nc.gpsimd.memset(src_raw[:, BQ - 1, :], 0).then_inc(pads, 1)
            nc.gpsimd.memset(dst_raw[:, BQ - 1, :], NPAD - 1).then_inc(pads, 1)
            nc.gpsimd.memset(epsln[:, :], LN_EPS).then_inc(const, 1)
            nc.gpsimd.memset(ident[:, :], 0.0).then_inc(const, 1)
            nc.gpsimd.memset(acc[:, :, N:NPAD], 0.0).then_inc(const, 1)
            pool.wait_ge(const, 3)
            nc.gpsimd.affine_select(out=ident[:, :], in_=ident[:, :], compare_op=ALU.not_equal, fill=1.0,
                                    base=0, pattern=[[-1, P]], channel_multiplier=1).then_inc(const, 1)

            def store(n, par):
                if not is_last(n):
                    after(pool, normed, n + 1, held)
                    pool.dma_start(group(nfull, n), xn[par][:, :, :]).then_inc(xln_out[par], 16)
                else:
                    pool.wait_ge(normed, n + 1)
                    for s, rows in row_tiles(n):
                        at = n * GROUP + s * P
                        pool.dma_start(xln_d[at:at + rows, :], xn[par][0:rows, s, :]).then_inc(xln_out[par], 16)

            over_steps(pool, store)
            pool.wait_ge(xln_out[0], 16 * (NT // 2 + len(row_tiles(LAST))))
            pool.wait_ge(xln_out[1], 16 * (NT // 2))

        @block.scalar
        def _(act):
            at = 0
            for name, c in VECS:
                act.dma_start(vraw[at:at + c, :], a[name].rearrange("(c p) -> c p", p=P)).then_inc(vec_in, 16)
                at += c
            act.dma_start(b1raw[:, :], a["L0_ffn_b1"].rearrange("e (c p) -> (e c) p", p=P)).then_inc(vec_in, 16)
            act.dma_start(ope[:, :], a["L0_gnn_eps"].rearrange("(o c) -> o c", o=1).to_broadcast([P, 1])).then_inc(eps_in, 16)
            act.dma_start(w1raw[:, :, :], a["L0_gnn_W1"].rearrange("(c p) m -> p c m", p=P)).then_inc(w_in, 16)
            act.wait_ge(w_in, 16)
            nc.scalar.copy(w1h[:, :, :], w1raw[:, :, :]).then_inc(w_high, 1)
            dview = ndst_t[:, :].rearrange("p (b j) -> p b j", j=CPB)
            for j in range(CPB):
                act.wait_ge(dst_turned, j + 1)
                nc.scalar.mul(dview[:, :, j], ps_e[j][:, 0:NBLK], -1.0).then_inc(dst_kept, 1)
            act.wait_ge(scaled, 1)

            def step(n, par):
                act.wait_ge(moments, n + 1)
                for s0, c, rows in row_parts(n):
                    last = nc.scalar.activation(rs[par][0:rows, s0:s0 + c], mv[par][0:rows, s0:s0 + c, 1], ACT.Sqrt,
                                                bias=epsln[0:rows, 0:1])
                last.then_inc(rooted, 1)
                cols = TAIL if is_last(n) else GROUP
                after(act, turned, n + 1, held)
                nc.scalar.activation(acc[:, :, bass.ds(n * GROUP, cols)], ps_x[par][:, :, 0:cols], ACT.Copy,
                                     scale=ope[:, 0:1]).then_inc(kept, 1)

            over_steps(act, step)

        @block.vector
        def _(dve):
            dve.wait_ge(edges_in, 16 * EDGE_LOADS)
            nc.vector.tensor_scalar(src_f[:, :, :], src_raw[:, :, :], 0.0, float(N - 1), ALU.max, ALU.min).then_inc(cast, 1)
            nc.vector.tensor_copy(dst_f[:, :, :], dst_raw[:, :, :]).then_inc(cast, 1)
            dve.wait_ge(cast, 2)
            nc.vector.tensor_reduce(reach_f[:, :, 0], dst_f[:, :, :], AX.X, ALU.min).then_inc(reached, 1)
            nc.vector.tensor_reduce(reach_f[:, :, 1], dst_f[:, :, :], AX.X, ALU.max).then_inc(reached, 1)
            dve.wait_ge(reached, 2)
            nc.vector.tensor_copy(reach[:, :, :], reach_f[:, :, :]).then_inc(shifted, 1)
            dve.wait_ge(shifted, 1)
            nc.vector.tensor_scalar(reach[:, :, :], reach[:, :, :], P.bit_length() - 1, None, ALU.arith_shift_right).then_inc(shifted, 1)
            dve.wait_ge(shifted, 2)
            nc.vector.tensor_scalar(reach[:, :, :], reach[:, :, :], 0.0, float(NTILES - 1), ALU.max, ALU.min).then_inc(shifted, 1)
            dve.wait_ge(shifted, 3)
            nc.vector.tensor_scalar(reach[:, :, 1], reach[:, :, 1], 1.0, None, ALU.add).then_inc(shifted, 1)
            dve.wait_ge(eps_in, 16)
            nc.vector.tensor_scalar(ope[:, :], ope[:, :], 1.0, None, ALU.add).then_inc(scaled, 1)
            sview = src_t[:, :].rearrange("p (b j) -> p b j", j=CPB)
            for j in range(CPB):
                dve.wait_ge(src_turned, j + 1)
                nc.vector.tensor_copy(sview[:, :, j], ps_e[j][:, 0:NBLK]).then_inc(src_kept, 1)
            dve.wait_ge(vec_turned, 1)
            nc.vector.tensor_copy(vec[:, :], ps_x[0][:, 0, 0:NVEC]).then_inc(vec_kept, 1)
            nc.vector.tensor_copy(b1e[:, :], ps_x[1][:, 0, 0:NB1]).then_inc(vec_kept, 1)

            def step(n, par):
                loads = len(row_tiles(n)) if is_last(n) else 1
                for s, rows in row_tiles(n):
                    if s == 0:
                        dve.wait_ge(x_in[par], (uses(n, par) - 1 + loads) * 16)
                    last = nc.vector.bn_stats(st[par][0:rows, s, :], xg[par][0:rows, s, :])
                last.then_inc(summed, 1)
                after(dve, summed, n + 1, held)
                for s, rows in row_tiles(n):
                    last = nc.vector.bn_aggr(mv[par][0:rows, s, :], st[par][0:rows, s, :])
                last.then_inc(moments, 1)
                dve.wait_ge(rooted, n + 1)
                for s0, c, rows in row_parts(n):
                    last = nc.vector.reciprocal(rs[par][0:rows, s0:s0 + c], rs[par][0:rows, s0:s0 + c])
                last.then_inc(inverse, 1)
                if not static(n) or n >= 2:
                    dve.wait_ge(turned, n - 1)
                    dve.wait_ge(xln_out[par], (uses(n, par) - 1) * 16)
                dve.wait_ge(inverse, n + 1)
                for s, rows in row_tiles(n):
                    last = nc.vector.tensor_scalar(xn[par][0:rows, s, :], xg[par][0:rows, s, :], mv[par][0:rows, s, 0:1],
                                                   rs[par][0:rows, s:s + 1], ALU.subtract, ALU.mult)
                last.then_inc(normed, 1)

            over_steps(dve, step)
            dve.wait_ge(w_high, 1)
            nc.vector.tensor_tensor(w1l[:, :, :], w1raw[:, :, :], w1h[:, :, :].bitcast(F32), ALU.subtract).then_inc(w_low, 1)

        @block.tensor
        def _(pe):
            pe.wait_ge(const, 4)
            pe.wait_ge(cast, 2)
            for j in range(CPB):
                for q in range(BQ):
                    last = pe.transpose(ps_e[j][:, q * BP:(q + 1) * BP], src_f[:, q, j * P:(j + 1) * P], ident[0:BP, 0:BP])
                last.then_inc(src_turned, 1)
            for j in range(CPB):
                pe.wait_ge(src_kept, j + 1)
                for q in range(BQ):
                    last = pe.transpose(ps_e[j][:, q * BP:(q + 1) * BP], dst_f[:, q, j * P:(j + 1) * P], ident[0:BP, 0:BP])
                last.then_inc(dst_turned, 1)
            pe.wait_ge(vec_in, 16 * (len(VECS) + 1))
            pe.transpose(ps_x[0][:, 0, 0:NVEC], vraw[:, :], ident[0:NVEC, 0:NVEC])
            pe.transpose(ps_x[1][:, 0, 0:NB1], b1raw[:, :], ident[0:NB1, 0:NB1]).then_inc(vec_turned, 1)
            pe.wait_ge(vec_kept, 2)

            def step(n, par):
                if not static(n) or n >= 2:
                    pe.wait_ge(kept, n - 1)
                pe.wait_ge(normed, n + 1)
                for h in range(2):
                    for s, rows in row_tiles(n):
                        last = pe.transpose(ps_x[par][:, h, s * P:s * P + rows], xn[par][0:rows, s, h * P:(h + 1) * P],
                                            ident[0:rows, 0:rows])
                last.then_inc(turned, 1)

            over_steps(pe, step)


def aggregate(nc, xln_d, buf_d, acc, src_t, ndst_t, trow):
    ctx = ExitStack()
    with ctx:
        def sb(name, shape, dt=F32):
            return ctx.enter_context(nc.sbuf_tensor("b_" + name, shape, dt))

        def sem(name):
            return ctx.enter_context(nc.semaphore("b_" + name))

        HALF = BODY // 2
        rows = sb("rows", [P, SLOTS, CPB, D])
        index = [sb(f"index{k}", [P, HALF * CPB], I32) for k in range(2)]
        nodes = sb("nodes", [P, NPAD], I16)
        away = sb("away", [P, EB])
        onehot = sb("onehot", [P, 2 * EB])
        one = sb("one", [P, 1])
        zeros = sb("zeros", [P, 1, D])
        ps = ctx.enter_context(nc.psum_tensor("b_ps", [P, 2 * 512], F32))

        const, held, zeroed = sem("const"), sem("held"), sem("zeroed")
        indexed = [sem(f"indexed{k}") for k in range(2)]
        gathered = [sem(f"gathered{k}") for k in range(SLOTS)]
        slot_free, product, added = sem("slot_free"), sem("product"), sem("added")
        apart, picked = sem("apart"), sem("picked")
        block = ctx.enter_context(nc.Block())

        def bounds(eng, i, name):
            regs = [eng.alloc_register(f"{name}{q}") for q in range(2 * BODY)]
            eng.load(regs, trow[0:1, bass.ds(i * (2 * BODY), 2 * BODY)])
            return [eng.snap(r, min_val=0, max_val=NTILES) for r in regs]

        @block.sync
        def _(sp):
            sp.wait_ge(const, 4)
            sp.dma_start(buf_d.rearrange("(p r) f -> p r f", p=P),
                         zeros[:, :, :].to_broadcast([P, BUFROWS // P, D])).then_inc(zeroed, 16)

            def stage(i, k):
                sp.dma_start(index[k][:, :], src_t[:, bass.ds((i * BODY + k * HALF) * CPB, HALF * CPB)]).then_inc(indexed[k], 16)

            stage(0, 0)
            stage(0, 1)
            with sp.Fori(1, NBLK // BODY) as i:
                for k in range(2):
                    sp.wait_ge(slot_free, SLOTS + i * BODY - BODY + (k + 1) * HALF)
                    stage(i, k)
            sp.wait_ge(zeroed, 16)

        @block.gpsimd
        def _(pool):
            nc.gpsimd.memset(zeros[:, :, :], 0.0).then_inc(const, 1)
            nc.gpsimd.memset(one[:, :], 1.0).then_inc(const, 1)
            nc.gpsimd.iota(nodes[:, :], pattern=[[1, NPAD]], base=0, channel_multiplier=0).then_inc(const, 1)
            nc.gpsimd.memset(away[:, 0:1], 0.0).then_inc(const, 1)
            with pool.Fori(0, NBLK // BODY) as i:
                for k in range(BODY):
                    if k % HALF == 0:
                        after(pool, indexed[k // HALF], i * 16 + 16, held)
                    after(pool, slot_free, i * BODY + k + 1, held)
                    for j in range(CPB):
                        at = (k % HALF) * CPB + j
                        pool.indirect_dma_start(rows[:, k % SLOTS, j, :], None, xln_d,
                                                bass.IndirectOffsetOnAxis(index[k // HALF][:, at:at + 1], 0)
                                                ).then_inc(gathered[k % SLOTS], 16)

        @block.scalar
        def _(act):
            act.wait_ge(const, 4)
            act.sem_inc(picked, 1)
            step = act.alloc_register("act_step")
            act.reg_mov(step, 0)
            with act.Fori(0, NBLK // BODY) as i:
                r = bounds(act, i, "act_b")
                for k in range(BODY):
                    with act.Fori(r[2 * k], r[2 * k + 1]) as t:
                        s = act.snap(step)
                        ring = act.snap((s % 2) * EB)
                        after(act, product, s + 1, held)
                        after(act, picked, s + 1, held)
                        for j in range(CPB):
                            last = nc.scalar.activation(away[:, j * P:(j + 1) * P], nodes[:, bass.ds(t * P, P)], ACT.Abs,
                                                        bias=ndst_t[:, bass.ds((i * BODY + k) * CPB + j, 1)])
                        last.then_inc(apart, 1)
                        after(act, apart, s + 1, held)
                        nc.scalar.activation(onehot[:, bass.ds(ring, EB)], away[:, :], ACT.Relu,
                                             scale=-1.0, bias=one[:, 0:1]).then_inc(picked, 1)
                        act.reg_add(step, step, 1)

        @block.tensor
        def _(pe):
            pe.sem_inc(slot_free, SLOTS)
            pe.sem_inc(product, 2)
            step = pe.alloc_register("pe_step")
            pe.reg_mov(step, 0)
            with pe.Fori(0, NBLK // BODY) as i:
                r = bounds(pe, i, "pe_b")
                for k in range(BODY):
                    after(pe, gathered[k % SLOTS], (i * (BODY // SLOTS) + k // SLOTS + 1) * (CPB * 16), held)
                    with pe.Fori(r[2 * k], r[2 * k + 1]):
                        s = pe.snap(step)
                        ring = pe.snap((s % 2) * 512)
                        after(pe, added, s + 1, held)
                        after(pe, picked, s + 2, held)
                        for h in range(2):
                            for j in range(CPB):
                                last = pe.matmul(ps[:, bass.ds(ring + h * P, P)], rows[:, k % SLOTS, j, h * P:(h + 1) * P],
                                                 onehot[:, bass.ds(ring + j * P, P)], start=(j == 0), stop=(j == CPB - 1))
                        last.then_inc(product, 1)
                        pe.reg_add(step, step, 1)
                    pe.drain().then_inc(slot_free, 1)

        @block.vector
        def _(dve):
            dve.sem_inc(added, 2)
            step = dve.alloc_register("dve_step")
            dve.reg_mov(step, 0)
            with dve.Fori(0, NBLK // BODY) as i:
                r = bounds(dve, i, "dve_b")
                for k in range(BODY):
                    with dve.Fori(r[2 * k], r[2 * k + 1]) as t:
                        s = dve.snap(step)
                        ring = dve.snap((s % 2) * 512)
                        after(dve, added, s + 2, held)
                        after(dve, product, s + 3, held)
                        nc.vector.tensor_tensor(acc[:, :, bass.ds(t * P, P)],
                                                ps[:, bass.ds(ring, 2 * P)].rearrange("p (h n) -> p h n", h=2),
                                                acc[:, :, bass.ds(t * P, P)], ALU.add).then_inc(added, 1)
                        dve.reg_add(step, step, 1)




def layer(nc, which, a, h_in, h_out, acc, stats, vec, epsln, w, wraw, nextw):
    K, M = CH[which - 1] // P, CH[which] // P
    normal = which > 1
    ctx = ExitStack()
    with ctx:
        tag = f"l{which}_"

        def sb(name, shape, dt=F32):
            return ctx.enter_context(nc.sbuf_tensor(tag + name, shape, dt))

        def sem(name):
            return ctx.enter_context(nc.semaphore(tag + name))

        bias_at = VCOL[f"L0_gnn_b{which}"]
        w = [x[:, :, :].rearrange("p c m -> p (c m)").rearrange("p (c m) -> p c m", c=K) for x in w]
        if normal:
            g_at, beta_at = VCOL[f"L0_gnn_g{which - 1}"], VCOL[f"L0_gnn_beta{which - 1}"]
            hin = [sb(f"hin{k}", [P, K, TILE]) for k in range(2)]
            ex = sb("ex", [P, K, TILE])
            mv = sb("mv", [P, K, 2])
            scale = sb("scale", [P, K])
            shift = sb("shift", [P, K])
            hin_v = h_in.rearrange("(m p) n -> p m n", p=P)
        zh = [sb(f"zh{k}", [P, K, TILE], F32R) for k in range(2)]
        zl = [sb(f"zl{k}", [P, K, TILE], F32R) for k in range(2)]
        hout = [sb(f"hout{k}", [P, M, TILE]) for k in range(2)]
        hout_v = h_out.rearrange("(m p) n -> p m n", p=P)
        ps = [ctx.enter_context(nc.psum_tensor(f"{tag}ps{k}", [P, 512], F32)) for k in range(8)]
        if nextw:
            nraw = nextw[1] if nextw[2] is None else sb("nraw", list(nextw[1].shape))

        held, bn_done, bn_root, bn_ready = sem("held"), sem("bn_done"), sem("bn_root"), sem("bn_ready")
        w_ready, next_in, next_split = sem("w_ready"), sem("next_in"), sem("next_split")
        loaded = [sem(f"loaded{k}") for k in range(2)]
        exped, bounded, active, high, low = sem("exped"), sem("bounded"), sem("active"), sem("high"), sem("low")
        product, biased, counted = sem("product"), sem("biased"), sem("counted")
        stored = [sem(f"stored{k}") for k in range(2)]
        block = ctx.enter_context(nc.Block())
        W_PARTS = 2 if wraw is not None else 0

        @block.sync
        def _(sp):
            if normal:
                def load(n, par):
                    if not static(n) or n >= 2:
                        sp.wait_ge(low, n - 1)
                    sp.dma_start(hin[par][:, :, :], hin_v[:, :, bass.ds(n * TILE, TILE)]).then_inc(loaded[par], 16)

                over_steps(sp, load)

        @block.gpsimd
        def _(pool):
            def store(n, par):
                after(pool, biased, n * M + M, held)
                pool.dma_start(hout_v[:, :, bass.ds(n * TILE, TILE)], hout[par][:, :, :]).then_inc(stored[par], 16)

            if nextw:
                pool.dma_start(nraw[:, :, :], nextw[0].rearrange("(c p) m -> p c m", p=P)).then_inc(next_in, 16)
                pool.wait_ge(next_in, 16)
                if nextw[2] is not None:
                    nc.gpsimd.tensor_copy(nextw[1][:, :, :], nraw[:, :, :]).then_inc(next_split, 1)
                    pool.wait_ge(next_split, 1)
                    nc.gpsimd.tensor_tensor(nextw[2][:, :, :], nraw[:, :, :], nextw[1][:, :, :].bitcast(F32),
                                            ALU.subtract).then_inc(next_split, 1)
            over_steps(pool, store)
            pool.wait_ge(stored[0], 16 * (NT // 2 + 1))
            pool.wait_ge(stored[1], 16 * (NT // 2))

        @block.scalar
        def _(act):
            if W_PARTS:
                nc.scalar.copy(w[0], wraw[:, :, :]).then_inc(w_ready, 1)
            if normal:
                act.wait_ge(bn_done, 1)
                nc.scalar.activation(scale[:, :], mv[:, :, 1], ACT.Sqrt, bias=epsln[:, 0:1]).then_inc(bn_root, 1)
                act.wait_ge(bn_ready, 3)

            def prep(n, par):
                if not static(n) or n >= 1:
                    act.wait_ge(active, n)
                act.wait_ge(loaded[par], uses(n, par) * 16)
                for c in range(K):
                    nc.scalar.activation(ex[:, c, :], hin[par][:, c, :], ACT.Exp, bias=shift[:, c:c + 1], scale=scale[:, c:c + 1])
                    last = nc.scalar.activation(hin[par][:, c, :], hin[par][:, c, :], ACT.Identity, bias=shift[:, c:c + 1],
                                                scale=scale[:, c:c + 1])
                last.then_inc(exped, 1)

            def finish(n, par):
                if not static(n) or n >= 2:
                    act.wait_ge(stored[par], (uses(n, par) - 1) * 16)
                    act.wait_ge(counted, n - 1)
                for m in range(M):
                    act.wait_ge(product, n * M + m + 1)
                    nc.scalar.activation(hout[par][:, m, :], ps[(par * M + m) % 8][:, 0:TILE], ACT.Identity,
                                         bias=vec[:, bias_at + m:bias_at + m + 1]).then_inc(biased, 1)

            def step(n, par):
                if normal and not is_last(n):
                    prep(n + 1, 1 - par)
                finish(n, par)

            if normal:
                prep(0, 0)
            over_steps(act, step)

        @block.vector
        def _(dve):
            if W_PARTS:
                dve.wait_ge(w_ready, 1)
                nc.vector.tensor_tensor(w[1], wraw[:, :, :],
                                        w[0].bitcast(F32), ALU.subtract).then_inc(w_ready, 1)
            if normal:
                for c in range(K):
                    last = nc.vector.bn_aggr(mv[:, c, :], stats[:, c, :, :].rearrange("p t s -> p (t s)"))
                last.then_inc(bn_done, 1)
                dve.wait_ge(bn_root, 1)
                nc.vector.reciprocal(scale[:, :], scale[:, :]).then_inc(bn_ready, 1)
                dve.wait_ge(bn_ready, 1)
                nc.vector.tensor_tensor(scale[:, :], scale[:, :], vec[:, g_at:g_at + K], ALU.mult).then_inc(bn_ready, 1)
                dve.wait_ge(bn_ready, 2)
                nc.vector.tensor_tensor(shift[:, :], scale[:, :], mv[:, :, 0], ALU.mult).then_inc(bn_done, 1)
                dve.wait_ge(bn_done, 2)
                nc.vector.tensor_tensor(shift[:, :], vec[:, beta_at:beta_at + K], shift[:, :], ALU.subtract).then_inc(bn_ready, 1)

            def prep(n, par):
                if normal:
                    dve.wait_ge(exped, n + 1)
                    nc.vector.tensor_scalar(ex[:, :, :], ex[:, :, :], 1.0, 0.0, ALU.subtract, ALU.min).then_inc(bounded, 1)
                    dve.wait_ge(bounded, n + 1)
                    nc.vector.tensor_tensor(hin[par][:, :, :], hin[par][:, :, :], ex[:, :, :], ALU.max).then_inc(active, 1)
                    z = hin[par][:, :, :]
                    dve.wait_ge(active, n + 1)
                else:
                    z = acc[:, :, bass.ds(n * TILE, TILE)]
                if not static(n) or n >= 2:
                    after(dve, product, n * M - M, held)
                nc.vector.tensor_copy(zh[par][:, :, :], z).then_inc(high, 1)
                dve.wait_ge(high, n + 1)
                nc.vector.tensor_tensor(zl[par][:, :, :], z, zh[par][:, :, :].bitcast(F32), ALU.subtract).then_inc(low, 1)

            def finish(n, par):
                after(dve, biased, n * M + M, held)
                for m in range(M):
                    last = nc.vector.bn_stats(stats[:, m, bass.ds(n, 1), :].rearrange("p o s -> p (o s)"), hout[par][:, m, :])
                last.then_inc(counted, 1)

            def step(n, par):
                if not is_last(n):
                    prep(n + 1, 1 - par)
                finish(n, par)

            prep(0, 0)
            over_steps(dve, step)

        @block.tensor
        def _(pe):
            if W_PARTS:
                pe.wait_ge(w_ready, W_PARTS)

            def step(n, par):
                pe.wait_ge(low, n + 1)
                for m in range(M):
                    if not static(n) or n * M + m >= 8:
                        pe.wait_ge(biased, n * M + (m + 1 - 8))
                    o = ps[(par * M + m) % 8][:, 0:TILE]
                    cols = slice(m * P, (m + 1) * P)
                    for c in range(K):
                        pe.matmul(o, w[0][:, c, cols], zh[par][:, c, :], start=(c == 0), stop=False)
                        pe.matmul(o, w[0][:, c, cols], zl[par][:, c, :], start=False, stop=False)
                        last = pe.matmul(o, w[1][:, c, cols], zh[par][:, c, :], start=False, stop=(c == K - 1))
                    last.then_inc(product, 1)

            over_steps(pe, step)


def last_layer(nc, a, h_in, x1_d, buf_d, stats, vec, epsln, ident, gidx, gate):
    K = CH[3] // P
    g_at, beta_at = VCOL["L0_gnn_g3"], VCOL["L0_gnn_beta3"]
    ctx = ExitStack()
    with ctx:
        def sb(name, shape, dt=F32):
            return ctx.enter_context(nc.sbuf_tensor("f_" + name, shape, dt))

        def sem(name):
            return ctx.enter_context(nc.semaphore("f_" + name))

        def two(name, shape, dt=F32):
            return [sb(f"{name}{k}", shape, dt) for k in range(2)]

        hin, zh, zl = two("hin", [P, K, GROUP]), two("zh", [P, K, GROUP], F32R), two("zl", [P, K, GROUP], F32R)
        ex = sb("ex", [P, K, GROUP])
        mv, scale, shift = sb("mv", [P, K, 2]), sb("scale", [P, K]), sb("shift", [P, K])
        xg, x1, xl = two("xg", [P, 4, D]), two("x1", [P, 4, D]), two("xl", [P, 4, D])
        xt = sb("xt", [P, 2, GROUP])
        b4 = sb("b4", [P, 1, D])
        w4raw, w4h, w4l = sb("w4raw", [P, K, D]), sb("w4h", [P, K, D], F32R), sb("w4l", [P, K, D], F32R)
        gw = sb("gw", [P, 2, NE])
        gb = sb("gb", [P, 1, NE])
        ones, upper = sb("ones", [P, P]), sb("upper", [P, P])
        place_m = sb("place_m", [P, 1, NE])
        st, rmv, rs = two("st", [P, 4, 6]), two("rmv", [P, 4, 2]), two("rs", [P, 4])
        logit, expd, cand, onehot, hits = (two("logit", [P, 4, NE]), two("expd", [P, 4, NE]), two("cand", [P, 4, NE]),
                                           two("onehot", [P, 4, NE]), two("hits", [P, 4, NE]))
        best, expert, total = two("best", [P, 4, 1]), two("expert", [P, 4, 1]), two("total", [P, 4])
        place, kept, home, away = (two("place", [P, 4]), two("kept", [P, 4]), two("home", [P, 4]), two("away", [P, 4]))
        near, prob = two("near", [P, 4]), two("prob", [P, 4])
        sidx = two("sidx", [P, 4], I32)
        here, before = sb("here", [P, NE]), two("before", [P, NE])
        ps_y = [ctx.enter_context(nc.psum_tensor(f"f_ps_y{k}", [P, 4, D], F32)) for k in range(2)]
        ps_t = ctx.enter_context(nc.psum_tensor("f_ps_t", [P, 2, GROUP], F32))
        ps_l = ctx.enter_context(nc.psum_tensor("f_ps_l", [P, 4, NE], F32))
        ps_c = ctx.enter_context(nc.psum_tensor("f_ps_c", [P, 4, NE], F32))

        held, bn_done, bn_root, bn_ready = sem("held"), sem("bn_done"), sem("bn_root"), sem("bn_ready")
        small_in, const, w_in, w_split = sem("small_in"), sem("const"), sem("w_in"), sem("w_split")
        loaded, x_in = [sem(f"loaded{k}") for k in range(2)], [sem(f"x_in{k}") for k in range(2)]
        exped, bounded, active, high, low = sem("exped"), sem("bounded"), sem("active"), sem("high"), sem("low")
        based, product, summed, counted, moments, rooted, inverse, normed = (
            sem("based"), sem("product"), sem("summed"), sem("counted"), sem("moments"), sem("rooted"),
            sem("inverse"), sem("normed"))
        turned, xt_kept, logits = sem("turned"), sem("xt_kept"), sem("logits")
        first, expl, placed, second = sem("first"), sem("expl"), sem("placed"), sem("second")
        x1_out, sent = [sem(f"x1_out{k}") for k in range(2)], [sem(f"sent{k}") for k in range(2)]
        ROUTE1, ROUTE2 = 9, 10
        block = ctx.enter_context(nc.Block())

        hin_v = h_in.rearrange("(m p) n -> p m n", p=P)
        xfull = a["x"][0:LAST * GROUP, :].rearrange("(g s p) f -> g p s f", s=4, p=P)
        x1full = x1_d[0:LAST * GROUP, :].rearrange("(g s p) f -> g p s f", s=4, p=P)

        def group(view, n):
            if static(n):
                return view[n]
            return view[bass.ds(n, 1)].rearrange("o p s f -> (o p) s f")

        def width(n):
            return TAIL if is_last(n) else GROUP

        def piped(eng, step):
            step(0, 0)
            step(1, 1)
            with eng.Fori(1, NT // 2 - 1) as i:
                step(i * 2, 0)
                step(i * 2 + 1, 1)
            for n in range(NT - 3, NT + 2):
                step(n, n % 2)

        def valid(n):
            return not static(n) or 0 <= n < NT

        @block.sync
        def _(sp):
            sp.dma_start(b4[:, 0, :], a["L0_gnn_b4"].rearrange("(o f) -> o f", o=1).to_broadcast([P, D])).then_inc(small_in, 16)
            sp.dma_start(gb[:, 0, :], a["L0_ffn_gate_b"].rearrange("(o f) -> o f", o=1).to_broadcast([P, NE])).then_inc(small_in, 16)
            sp.dma_start(gw[:, :, :], a["L0_ffn_gate_w"].rearrange("(c p) e -> p c e", p=P)).then_inc(small_in, 16)

            def load(n, par):
                if not static(n) or n >= 2:
                    sp.wait_ge(low, n - 1)
                sp.dma_start(hin[par][:, :, 0:width(n)], hin_v[:, :, bass.ds(n * GROUP, width(n))]).then_inc(loaded[par], 16)
                if not static(n) or n >= 2:
                    sp.wait_ge(summed, n - 1)
                if not is_last(n):
                    sp.dma_start(xg[par][:, :, :], group(xfull, n)).then_inc(x_in[par], 16)
                else:
                    for s, rows in row_tiles(n):
                        at = n * GROUP + s * P
                        sp.dma_start(xg[par][0:rows, s, :], a["x"][at:at + rows, :]).then_inc(x_in[par], 16)

            over_steps(sp, load)

        @block.gpsimd
        def _(pool):
            pool.dma_start(w4raw[:, :, :], a["L0_gnn_W4"].rearrange("(c p) m -> p c m", p=P)).then_inc(w_in, 16)
            nc.gpsimd.memset(ones[:, :], 1.0).then_inc(const, 1)
            pool.wait_ge(const, 1)
            nc.gpsimd.affine_select(out=upper[:, :], in_=ones[:, :], compare_op=ALU.is_gt, fill=0.0,
                                    base=0, pattern=[[1, P]], channel_multiplier=-1).then_inc(const, 1)
            pool.wait_ge(w_in, 16)
            nc.gpsimd.tensor_copy(w4h[:, :, :], w4raw[:, :, :]).then_inc(w_split, 1)
            pool.wait_ge(w_split, 1)
            nc.gpsimd.tensor_tensor(w4l[:, :, :], w4raw[:, :, :], w4h[:, :, :].bitcast(F32), ALU.subtract).then_inc(w_split, 1)
            for e in range(NE):
                nc.gpsimd.memset(place_m[:, :, e:e + 1], float(e - NE)).then_inc(const, 1)
            nc.gpsimd.memset(before[0][:, :], 0.0).then_inc(const, 1)
            pool.wait_ge(small_in, 48)

            def base(n, par):
                loads = len(row_tiles(n)) if is_last(n) else 1
                pool.wait_ge(x_in[par], (uses(n, par) - 1 + loads) * 16)
                for s0, c, rows in row_parts(n):
                    last = nc.gpsimd.tensor_tensor(xg[par][0:rows, s0:s0 + c, :], xg[par][0:rows, s0:s0 + c, :],
                                                   b4[0:rows, :, :].to_broadcast([rows, c, D]), ALU.add)
                last.then_inc(based, 1)

            def step(n, par):
                if valid(n):
                    if not is_last(n):
                        base(n + 1, 1 - par)
                        after(pool, summed, n + 1, held)
                        pool.dma_start(group(x1full, n), x1[par][:, :, :]).then_inc(x1_out[par], 16)
                    else:
                        pool.wait_ge(summed, n + 1)
                        for s, rows in row_tiles(n):
                            at = n * GROUP + s * P
                            pool.dma_start(x1_d[at:at + rows, :], x1[par][0:rows, s, :]).then_inc(x1_out[par], 16)
                m = n - 2
                if valid(m):
                    after(pool, second, m * ROUTE2 + ROUTE2, held)
                    for s, rows in row_tiles(m):
                        pool.indirect_dma_start(buf_d, bass.IndirectOffsetOnAxis(sidx[par][0:rows, s:s + 1], 0),
                                                xl[par][0:rows, s, :], None, bounds_check=NE * CAP - 1,
                                                oob_is_err=False).then_inc(sent[par], 16)

            base(0, 0)
            piped(pool, step)
            tail = len(row_tiles(LAST))
            pool.wait_ge(x1_out[0], 16 * (NT // 2 + tail))
            pool.wait_ge(x1_out[1], 16 * (NT // 2))
            pool.wait_ge(sent[0], 16 * (4 * (NT // 2) + tail))
            pool.wait_ge(sent[1], 16 * 4 * (NT // 2))

        @block.scalar
        def _(act):
            act.wait_ge(bn_done, 1)
            nc.scalar.activation(scale[:, :], mv[:, :, 1], ACT.Sqrt, bias=epsln[:, 0:1]).then_inc(bn_root, 1)
            act.wait_ge(bn_ready, 3)

            def prep(n, par):
                w = width(n)
                if not static(n) or n >= 1:
                    act.wait_ge(active, n)
                act.wait_ge(loaded[par], uses(n, par) * 16)
                for c in range(K):
                    nc.scalar.activation(ex[:, c, 0:w], hin[par][:, c, 0:w], ACT.Exp, bias=shift[:, c:c + 1], scale=scale[:, c:c + 1])
                    last = nc.scalar.activation(hin[par][:, c, 0:w], hin[par][:, c, 0:w], ACT.Identity, bias=shift[:, c:c + 1],
                                                scale=scale[:, c:c + 1])
                last.then_inc(exped, 1)

            def step(n, par):
                if valid(n):
                    if not is_last(n):
                        prep(n + 1, 1 - par)
                    act.wait_ge(moments, n + 1)
                    for s0, c, rows in row_parts(n):
                        last = nc.scalar.activation(rs[par][0:rows, s0:s0 + c], rmv[par][0:rows, s0:s0 + c, 1], ACT.Sqrt,
                                                    bias=epsln[0:rows, 0:1])
                    last.then_inc(rooted, 1)
                    if not static(n) or n >= 1:
                        act.wait_ge(logits, n)
                    act.wait_ge(turned, n + 1)
                    nc.scalar.copy(xt[:, :, 0:width(n)], ps_t[:, :, 0:width(n)]).then_inc(xt_kept, 1)
                m, mpar = n - 1, 1 - par
                if valid(m):
                    act.wait_ge(first, m * ROUTE1 + 3)
                    for s0, c, rows in row_parts(m):
                        last = nc.scalar.activation(expd[mpar][0:rows, s0:s0 + c, :], logit[mpar][0:rows, s0:s0 + c, :], ACT.Exp)
                    last.then_inc(expl, 1)

            prep(0, 0)
            piped(act, step)

        @block.vector
        def _(dve):
            for c in range(K):
                last = nc.vector.bn_aggr(mv[:, c, :], stats[:, c, :, :].rearrange("p t s -> p (t s)"))
            last.then_inc(bn_done, 1)
            dve.wait_ge(bn_root, 1)
            nc.vector.reciprocal(scale[:, :], scale[:, :]).then_inc(bn_ready, 1)
            dve.wait_ge(bn_ready, 1)
            nc.vector.tensor_tensor(scale[:, :], scale[:, :], vec[:, g_at:g_at + K], ALU.mult).then_inc(bn_ready, 1)
            dve.wait_ge(bn_ready, 2)
            nc.vector.tensor_tensor(shift[:, :], scale[:, :], mv[:, :, 0], ALU.mult).then_inc(bn_done, 1)
            dve.wait_ge(bn_done, 2)
            nc.vector.tensor_tensor(shift[:, :], vec[:, beta_at:beta_at + K], shift[:, :], ALU.subtract).then_inc(bn_ready, 1)
            dve.wait_ge(const, NE + 3)
            dve.wait_ge(small_in, 48)

            def prep(n, par):
                w = width(n)
                dve.wait_ge(exped, n + 1)
                nc.vector.tensor_scalar(ex[:, :, 0:w], ex[:, :, 0:w], 1.0, 0.0, ALU.subtract, ALU.min).then_inc(bounded, 1)
                dve.wait_ge(bounded, n + 1)
                nc.vector.tensor_tensor(hin[par][:, :, 0:w], hin[par][:, :, 0:w], ex[:, :, 0:w], ALU.max).then_inc(active, 1)
                if not static(n) or n >= 2:
                    after(dve, product, n - 1, held)
                dve.wait_ge(active, n + 1)
                nc.vector.tensor_copy(zh[par][:, :, 0:w], hin[par][:, :, 0:w]).then_inc(high, 1)
                dve.wait_ge(high, n + 1)
                nc.vector.tensor_tensor(zl[par][:, :, 0:w], hin[par][:, :, 0:w], zh[par][:, :, 0:w].bitcast(F32),
                                        ALU.subtract).then_inc(low, 1)

            def norm(n, par):
                if not static(n) or n >= 2:
                    dve.wait_ge(x1_out[par], (uses(n, par) - 1) * 16)
                dve.wait_ge(based, n + 1)
                dve.wait_ge(product, n + 1)
                for s0, c, rows in row_parts(n):
                    last = nc.vector.tensor_tensor(x1[par][0:rows, s0:s0 + c, :], ps_y[par][0:rows, s0:s0 + c, :],
                                                   xg[par][0:rows, s0:s0 + c, :], ALU.add)
                last.then_inc(summed, 1)
                dve.wait_ge(summed, n + 1)
                for s, rows in row_tiles(n):
                    last = nc.vector.bn_stats(st[par][0:rows, s, :], x1[par][0:rows, s, :])
                last.then_inc(counted, 1)
                after(dve, counted, n + 1, held)
                for s, rows in row_tiles(n):
                    last = nc.vector.bn_aggr(rmv[par][0:rows, s, :], st[par][0:rows, s, :])
                last.then_inc(moments, 1)
                dve.wait_ge(rooted, n + 1)
                for s0, c, rows in row_parts(n):
                    last = nc.vector.reciprocal(rs[par][0:rows, s0:s0 + c], rs[par][0:rows, s0:s0 + c])
                last.then_inc(inverse, 1)
                if not static(n) or n >= 2:
                    dve.wait_ge(turned, n - 1)
                    dve.wait_ge(sent[par], (uses(n, par) - 1) * 64)
                dve.wait_ge(inverse, n + 1)
                for s, rows in row_tiles(n):
                    last = nc.vector.tensor_scalar(xl[par][0:rows, s, :], x1[par][0:rows, s, :], rmv[par][0:rows, s, 0:1],
                                                   rs[par][0:rows, s:s + 1], ALU.subtract, ALU.mult)
                last.then_inc(normed, 1)

            def choose(n, par):
                def done(k):
                    dve.wait_ge(first, n * ROUTE1 + k)

                parts = row_parts(n)
                dve.wait_ge(logits, n + 1)
                for s0, c, rows in parts:
                    last = nc.vector.tensor_tensor(logit[par][0:rows, s0:s0 + c, :], ps_l[0:rows, s0:s0 + c, :],
                                                   gb[0:rows, :, :].to_broadcast([rows, c, NE]), ALU.add)
                last.then_inc(first, 1)
                done(1)
                for s0, c, rows in parts:
                    last = nc.vector.tensor_reduce(best[par][0:rows, s0:s0 + c, 0], logit[par][0:rows, s0:s0 + c, :], AX.X, ALU.max)
                last.then_inc(first, 1)
                done(2)
                for s0, c, rows in parts:
                    last = nc.vector.tensor_tensor(logit[par][0:rows, s0:s0 + c, :], logit[par][0:rows, s0:s0 + c, :],
                                                   best[par][0:rows, s0:s0 + c, :].to_broadcast([rows, c, NE]), ALU.subtract)
                last.then_inc(first, 1)
                done(3)
                for s0, c, rows in parts:
                    last = nc.vector.tensor_scalar(cand[par][0:rows, s0:s0 + c, :], logit[par][0:rows, s0:s0 + c, :], 0.0, None, ALU.is_ge)
                last.then_inc(first, 1)
                done(4)
                for s0, c, rows in parts:
                    last = nc.vector.tensor_tensor(cand[par][0:rows, s0:s0 + c, :], cand[par][0:rows, s0:s0 + c, :],
                                                   place_m[0:rows, :, :].to_broadcast([rows, c, NE]), ALU.mult)
                last.then_inc(first, 1)
                done(5)
                for s0, c, rows in parts:
                    last = nc.vector.tensor_reduce(expert[par][0:rows, s0:s0 + c, 0], cand[par][0:rows, s0:s0 + c, :], AX.X, ALU.min)
                last.then_inc(first, 1)
                done(6)
                for s0, c, rows in parts:
                    last = nc.vector.tensor_tensor(onehot[par][0:rows, s0:s0 + c, :], place_m[0:rows, :, :].to_broadcast([rows, c, NE]),
                                                   expert[par][0:rows, s0:s0 + c, :].to_broadcast([rows, c, NE]), ALU.is_equal)
                last.then_inc(first, 1)
                done(7)
                rows = parts[-1][2] if is_last(n) else P
                nc.vector.tensor_reduce(here[0:rows, :], onehot[par][0:rows, 0:len(row_tiles(n)), :].rearrange("p s e -> p e s"),
                                        AX.X, ALU.add).then_inc(first, 1)
                done(8)
                nc.vector.tensor_tensor(before[1 - par][0:rows, :], before[par][0:rows, :], here[0:rows, :], ALU.add).then_inc(first, 1)

            def assign(n, par):
                def done(k):
                    dve.wait_ge(second, n * ROUTE2 + k)

                parts = row_parts(n)
                dve.wait_ge(expl, n + 1)
                for s0, c, rows in parts:
                    last = nc.vector.tensor_reduce(total[par][0:rows, s0:s0 + c], expd[par][0:rows, s0:s0 + c, :], AX.X, ALU.add)
                last.then_inc(second, 1)
                dve.wait_ge(placed, n + 1)
                for s0, c, rows in parts:
                    last = nc.vector.tensor_tensor(hits[par][0:rows, s0:s0 + c, :], ps_c[0:rows, s0:s0 + c, :],
                                                   onehot[par][0:rows, s0:s0 + c, :], ALU.mult)
                last.then_inc(second, 1)
                done(1)
                for s0, c, rows in parts:
                    last = nc.vector.reciprocal(prob[par][0:rows, s0:s0 + c], total[par][0:rows, s0:s0 + c])
                last.then_inc(second, 1)
                done(2)
                for s0, c, rows in parts:
                    nc.vector.tensor_reduce(place[par][0:rows, s0:s0 + c], hits[par][0:rows, s0:s0 + c, :], AX.X, ALU.add)
                    last = nc.vector.tensor_scalar(home[par][0:rows, s0:s0 + c], expert[par][0:rows, s0:s0 + c, 0], float(CAP),
                                                   float(NE * CAP), ALU.mult, ALU.add)
                last.then_inc(second, 1)
                done(4)
                for s0, c, rows in parts:
                    nc.vector.tensor_scalar(kept[par][0:rows, s0:s0 + c], place[par][0:rows, s0:s0 + c], float(CAP), None, ALU.is_lt)
                    nc.vector.tensor_scalar(away[par][0:rows, s0:s0 + c], place[par][0:rows, s0:s0 + c], float(CAP), float(FAR),
                                            ALU.is_ge, ALU.mult)
                    last = nc.vector.tensor_scalar(near[par][0:rows, s0:s0 + c], place[par][0:rows, s0:s0 + c], float(CAP - 1), None, ALU.min)
                last.then_inc(second, 1)
                done(5)
                for s0, c, rows in parts:
                    nc.vector.tensor_tensor(gate[0:rows, bass.ds(n * 4 + s0, c)], prob[par][0:rows, s0:s0 + c],
                                            kept[par][0:rows, s0:s0 + c], ALU.mult)
                    nc.vector.tensor_tensor(near[par][0:rows, s0:s0 + c], near[par][0:rows, s0:s0 + c], home[par][0:rows, s0:s0 + c], ALU.add)
                    last = nc.vector.tensor_tensor(place[par][0:rows, s0:s0 + c], place[par][0:rows, s0:s0 + c],
                                                   home[par][0:rows, s0:s0 + c], ALU.add)
                last.then_inc(second, 1)
                done(6)
                for s0, c, rows in parts:
                    last = nc.vector.tensor_tensor(away[par][0:rows, s0:s0 + c], away[par][0:rows, s0:s0 + c],
                                                   place[par][0:rows, s0:s0 + c], ALU.add)
                last.then_inc(second, 1)
                done(7)
                for s0, c, rows in parts:
                    last = nc.vector.tensor_scalar(gidx[0:rows, bass.ds(n * 4 + s0, c)], near[par][0:rows, s0:s0 + c], 0.0, None, ALU.add)
                last.then_inc(second, 1)
                for s0, c, rows in parts:
                    last = nc.vector.tensor_copy(sidx[par][0:rows, s0:s0 + c], away[par][0:rows, s0:s0 + c])
                last.then_inc(second, 1)
                done(9)
                dve.sem_inc(second, 1)

            def step(n, par):
                if valid(n - 2):
                    assign(n - 2, par)
                if valid(n):
                    if not is_last(n):
                        prep(n + 1, 1 - par)
                    norm(n, par)
                if valid(n - 1):
                    choose(n - 1, 1 - par)

            prep(0, 0)
            piped(dve, step)

        @block.tensor
        def _(pe):
            pe.wait_ge(small_in, 48)
            pe.wait_ge(const, NE + 3)
            pe.wait_ge(w_split, 2)

            def rows_of(n, par):
                pe.wait_ge(low, n + 1)
                if not static(n) or n >= 2:
                    pe.wait_ge(summed, n - 1)
                for s, rows in row_tiles(n):
                    o = ps_y[par][0:rows, s, :]
                    cols = slice(s * P, s * P + rows)
                    for c in range(K):
                        pe.matmul(o, zh[par][:, c, cols], w4h[:, c, :], start=(c == 0), stop=False)
                        pe.matmul(o, zh[par][:, c, cols], w4l[:, c, :], start=False, stop=False)
                        last = pe.matmul(o, zl[par][:, c, cols], w4h[:, c, :], start=False, stop=(c == K - 1))
                last.then_inc(product, 1)

            def turn(n, par):
                if not static(n) or n >= 1:
                    pe.wait_ge(xt_kept, n)
                pe.wait_ge(normed, n + 1)
                for h in range(2):
                    for s, rows in row_tiles(n):
                        last = pe.transpose(ps_t[:, h, s * P:s * P + rows], xl[par][0:rows, s, h * P:(h + 1) * P], ident[0:rows, 0:rows])
                last.then_inc(turned, 1)

            def score(n):
                if not static(n) or n >= 1:
                    pe.wait_ge(first, n * ROUTE1 - ROUTE1 + 1)
                pe.wait_ge(xt_kept, n + 1)
                for s, rows in row_tiles(n):
                    for h in range(2):
                        last = pe.matmul(ps_l[0:rows, s, :], xt[:, h, s * P:s * P + rows], gw[:, h, :], start=(h == 0), stop=(h == 1))
                last.then_inc(logits, 1)

            def count(n, par):
                if not static(n) or n >= 1:
                    pe.wait_ge(second, n * ROUTE2 - ROUTE2 + 2)
                pe.wait_ge(first, n * ROUTE1 + ROUTE1)
                for s, rows in row_tiles(n):
                    o = ps_c[0:rows, s, :]
                    pe.matmul(o, ones[:, 0:rows], before[par][:, :], start=True, stop=False)
                    for t in range(s):
                        pe.matmul(o, ones[:, 0:rows], onehot[par][:, t, :], start=False, stop=False)
                    last = pe.matmul(o, upper[0:rows, 0:rows], onehot[par][0:rows, s, :], start=False, stop=True)
                last.then_inc(placed, 1)

            def step(n, par):
                if valid(n):
                    rows_of(n, par)
                    turn(n, par)
                    score(n)
                if valid(n - 1):
                    count(n - 1, 1 - par)

            piped(pe, step)


def experts(nc, a, buf_d, y_d, ident, b1e):
    ctx = ExitStack()
    with ctx:
        def sb(name, shape, dt=F32):
            return ctx.enter_context(nc.sbuf_tensor("g_" + name, shape, dt))

        def sem(name):
            return ctx.enter_context(nc.semaphore("g_" + name))

        def two(name, shape, dt=F32):
            return [sb(f"{name}{k}", shape, dt) for k in range(2)]

        FC, DC = F // P, D // P
        w1raw, w2raw = two("w1raw", [P, DC, F]), two("w2raw", [P, FC, D])
        w1h, w1l = two("w1h", [P, DC, F], F32R), two("w1l", [P, DC, F], F32R)
        w2h, w2l = two("w2h", [P, FC, D], F32R), two("w2l", [P, FC, D], F32R)
        b2 = two("b2", [P, 1, D])
        xin = two("xin", [P, 4, D])
        xh, xl = two("xh", [P, DC, GROUP], F32R), two("xl", [P, DC, GROUP], F32R)
        hid = sb("hid", [P, FC, GROUP])
        hh, hl = sb("hh", [P, FC, GROUP], F32R), sb("hl", [P, FC, GROUP], F32R)
        ysb = two("ysb", [P, 4, D])
        ps_t = ctx.enter_context(nc.psum_tensor("g_ps_t", [P, DC, GROUP], F32))
        ps_h = [ctx.enter_context(nc.psum_tensor(f"g_ps_h{k}", [P, GROUP], F32)) for k in range(4)]
        ps_y = ctx.enter_context(nc.psum_tensor("g_ps_y", [P, 4, D], F32))

        held = sem("held")
        w_in, w_high, w_split = [sem(f"w_in{k}") for k in range(2)], sem("w_high"), sem("w_split")
        x_in = [sem(f"x_in{k}") for k in range(2)]
        turned, hidden, y_ready, y_free = sem("turned"), sem("hidden"), sem("y_ready"), sem("y_free")
        x_high, x_low, up, hid_low, down, y_out = (sem("x_high"), sem("x_low"), sem("up"), sem("hid_low"),
                                                   sem("down"), sem("y_out"))
        block = ctx.enter_context(nc.Block())
        TPE = len(XT)

        def tiles(q):
            return [(s, min(P, XT[q] - s * P)) for s in range(-(-XT[q] // P))]

        def parts(q):
            full, rest = divmod(XT[q], P)
            return [(0, full, P)] + ([(full, 1, rest)] if rest else [])

        def loads_to(q):
            return sum(len(parts(k)) for k in range(q % 2, q + 1, 2))

        def loads_each(par):
            return sum(len(parts(k)) for k in range(par, TPE, 2))

        def stores_to(q):
            return sum(len(parts(k)) for k in range(q + 1))

        def over_tiles(eng, tile):
            with eng.Fori(0, NE // 2) as i:
                for u in range(2 * TPE):
                    tile(i * (2 * TPE) + u, i * 2 + u // TPE, u // TPE, u % TPE)

        def rows_of(base, at, q, s0, c, rows):
            return base[bass.ds(at + s0 * P, c * rows), :].rearrange("(s p) f -> p s f", p=rows)

        @block.sync
        def _(sp):
            def load(e, q):
                for s0, c, rows in parts(q):
                    sp.dma_start(xin[q % 2][0:rows, s0:s0 + c, :],
                                 rows_of(buf_d, e * CAP + q * GROUP, q, s0, c, rows)).then_inc(x_in[q % 2], 16)

            def tile(t, e, k, q):
                sp.wait_ge(turned, t + 2)
                load(e + (q + 1) // TPE, (q + 1) % TPE)
                sp.wait_ge(y_ready, t + 2)
                for s0, c, rows in parts(q):
                    sp.dma_start(rows_of(y_d, e * CAP + q * GROUP, q, s0, c, rows), ysb[q % 2][0:rows, s0:s0 + c, :]).then_inc(y_out, 16)
                sp.wait_ge(y_out, e * (16 * stores_to(TPE - 1)) + 16 * stores_to(q))
                sp.sem_inc(y_free, 1)

            load(0, 0)
            over_tiles(sp, tile)
            sp.wait_ge(x_in[0], 16 * (NE * loads_each(0) + len(parts(0))))

        @block.gpsimd
        def _(pool):
            pool.sem_inc(y_free, 2)

            def weights(e, k):
                if not static(e):
                    after(pool, y_ready, e * TPE - TPE + 1, held)
                o = "o p c m -> p (o c) m"
                pool.dma_start(w1raw[k][:, :, :], a["L0_ffn_w1"][bass.ds(e, 1)].rearrange("o (c p) m -> o p c m", p=P).rearrange(o)).then_inc(w_in[k], 16)
                pool.dma_start(w2raw[k][:, :, :], a["L0_ffn_w2"][bass.ds(e, 1)].rearrange("o (c p) m -> o p c m", p=P).rearrange(o)).then_inc(w_in[k], 16)
                pool.dma_start(b2[k][:, 0, :], a["L0_ffn_b2"][bass.ds(e, 1), :].to_broadcast([P, D])).then_inc(w_in[k], 16)
                after(pool, w_in[k], uses(e, k) * 48, held)
                nc.gpsimd.tensor_copy(w1h[k][:, :, :], w1raw[k][:, :, :])
                nc.gpsimd.tensor_copy(w2h[k][:, :, :], w2raw[k][:, :, :]).then_inc(w_high, 1)
                after(pool, w_high, e + 1, held)
                nc.gpsimd.tensor_tensor(w1l[k][:, :, :], w1raw[k][:, :, :], w1h[k][:, :, :].bitcast(F32), ALU.subtract)
                nc.gpsimd.tensor_tensor(w2l[k][:, :, :], w2raw[k][:, :, :], w2h[k][:, :, :].bitcast(F32), ALU.subtract).then_inc(w_split, 1)

            weights(0, 0)
            weights(1, 1)
            with pool.Fori(1, NE // 2) as i:
                for k in range(2):
                    weights(i * 2 + k, k)

        @block.scalar
        def _(act):
            act.sem_inc(hidden, 4)

            def high(t, q):
                act.wait_ge(turned, t + 3)
                nc.scalar.copy(xh[q % 2][:, :, 0:XT[q]], ps_t[:, :, 0:XT[q]]).then_inc(x_high, 1)

            def tile(t, e, k, q):
                for f in range(FC):
                    b = b1e[:, bass.ds(e * FC + f, 1)]
                    after(act, up, t * FC + f + 1, held)
                    nc.scalar.activation(hid[:, f, 0:XT[q]], ps_h[f % 4][:, 0:XT[q]], ACT.Relu, bias=b)
                    nc.scalar.activation(hh[:, f, 0:XT[q]], ps_h[f % 4][:, 0:XT[q]], ACT.Relu, bias=b).then_inc(hidden, 1)
                high(t + 1, (q + 1) % TPE)

            high(0, 0)
            over_tiles(act, tile)

        @block.vector
        def _(dve):
            dve.sem_inc(y_ready, 1)

            def rest(t, q):
                dve.wait_ge(x_high, t + 1)
                nc.vector.tensor_tensor(xl[q % 2][:, :, 0:XT[q]], ps_t[:, :, 0:XT[q]], xh[q % 2][:, :, 0:XT[q]].bitcast(F32),
                                        ALU.subtract).then_inc(x_low, 1)

            def tile(t, e, k, q):
                for f in range(FC):
                    dve.wait_ge(hidden, t * FC + f + 5)
                    nc.vector.tensor_tensor(hl[:, f, 0:XT[q]], hid[:, f, 0:XT[q]], hh[:, f, 0:XT[q]].bitcast(F32),
                                            ALU.subtract).then_inc(hid_low, 1)
                rest(t + 1, (q + 1) % TPE)
                dve.wait_ge(y_free, t + 1)
                dve.wait_ge(down, t + 1)
                for s0, c, rows in parts(q):
                    last = nc.vector.tensor_tensor(ysb[q % 2][0:rows, s0:s0 + c, :], ps_y[0:rows, s0:s0 + c, :],
                                                   b2[k][0:rows, :, :].to_broadcast([rows, c, D]), ALU.add)
                last.then_inc(y_ready, 1)

            rest(0, 0)
            over_tiles(dve, tile)

        @block.tensor
        def _(pe):
            pe.sem_inc(turned, 2)

            def turn(e, q):
                pe.wait_ge(x_in[q % 2], e * (16 * loads_each(q % 2)) + 16 * loads_to(q))
                for h in range(DC):
                    for s, rows in tiles(q):
                        last = pe.transpose(ps_t[:, h, s * P:s * P + rows], xin[q % 2][0:rows, s, h * P:(h + 1) * P], ident[0:rows, 0:rows])
                last.then_inc(turned, 1)

            def tile(t, e, k, q):
                if q == 0:
                    pe.wait_ge(w_split, e + 1)
                pe.wait_ge(x_low, t + 1)
                for f in range(FC):
                    pe.wait_ge(hidden, t * FC + f + 1)
                    o = ps_h[f % 4][:, 0:XT[q]]
                    cols = slice(f * P, (f + 1) * P)
                    for c in range(DC):
                        pe.matmul(o, w1h[k][:, c, cols], xh[q % 2][:, c, 0:XT[q]], start=(c == 0), stop=False)
                        pe.matmul(o, w1h[k][:, c, cols], xl[q % 2][:, c, 0:XT[q]], start=False, stop=False)
                        last = pe.matmul(o, w1l[k][:, c, cols], xh[q % 2][:, c, 0:XT[q]], start=False, stop=(c == DC - 1))
                    last.then_inc(up, 1)
                turn(e + (q + 1) // TPE, (q + 1) % TPE)
                pe.wait_ge(y_ready, t + 1)
                for s, rows in tiles(q):
                    o = ps_y[0:rows, s, :]
                    cols = slice(s * P, s * P + rows)
                    for f in range(FC):
                        if s == 0:
                            pe.wait_ge(hid_low, t * FC + f + 1)
                        pe.matmul(o, hh[:, f, cols], w2h[k][:, f, :], start=(f == 0), stop=False)
                        pe.matmul(o, hh[:, f, cols], w2l[k][:, f, :], start=False, stop=False)
                        last = pe.matmul(o, hl[:, f, cols], w2h[k][:, f, :], start=False, stop=(f == FC - 1))
                last.then_inc(down, 1)

            turn(0, 0)
            over_tiles(pe, tile)


def combine(nc, x1_d, y_d, gidx, gate, out):
    ctx = ExitStack()
    with ctx:
        def sb(name, shape, dt=F32):
            return ctx.enter_context(nc.sbuf_tensor("h_" + name, shape, dt))

        def sem(name):
            return ctx.enter_context(nc.semaphore("h_" + name))

        def two(name, shape, dt=F32):
            return [sb(f"{name}{k}", shape, dt) for k in range(2)]

        index = two("index", [P, 4], I32)
        factor = two("factor", [P, 4])
        y, xr, odd, above, below = (two("y", [P, 4, D]), two("xr", [P, 4, D]), sb("odd", [P, 4, D]), sb("above", [P, 4, D]),
                                    sb("below", [P, 4, D]))
        held, staged = sem("held"), sem("staged")
        y_in, x_in = [sem(f"y_in{k}") for k in range(2)], [sem(f"x_in{k}") for k in range(2)]
        gated, split, joined, cleaned, mixed = sem("gated"), sem("split"), sem("joined"), sem("cleaned"), sem("mixed")
        stored = [sem(f"stored{k}") for k in range(2)]
        block = ctx.enter_context(nc.Block())
        x1full = x1_d[0:LAST * GROUP, :].rearrange("(g s p) f -> g p s f", s=4, p=P)
        outfull = out[0:LAST * GROUP, :].rearrange("(g s p) f -> g p s f", s=4, p=P)

        def group(view, n):
            if static(n):
                return view[n]
            return view[bass.ds(n, 1)].rearrange("o p s f -> (o p) s f")

        @block.sync
        def _(sp):
            def load(n, par):
                if not static(n) or n >= 2:
                    sp.wait_ge(stored[par], (uses(n, par) - 1) * 16)
                if not is_last(n):
                    sp.dma_start(xr[par][:, :, :], group(x1full, n)).then_inc(x_in[par], 16)
                else:
                    for s, rows in row_tiles(n):
                        at = n * GROUP + s * P
                        sp.dma_start(xr[par][0:rows, s, :], x1_d[at:at + rows, :]).then_inc(x_in[par], 16)

            over_steps(sp, load)

        @block.gpsimd
        def _(pool):
            def step(n, par):
                after(pool, staged, n + 1, held)
                for s, rows in row_tiles(n):
                    pool.indirect_dma_start(y[par][0:rows, s, :], None, y_d,
                                            bass.IndirectOffsetOnAxis(index[par][0:rows, s:s + 1], 0)).then_inc(y_in[par], 16)

            over_steps(pool, step)

        @block.scalar
        def _(act):
            def step(n, par):
                act.wait_ge(y_in[par], 64 * (uses(n, par) - 1) + 16 * len(row_tiles(n)))
                act.wait_ge(staged, n + 1)
                for s, rows in row_tiles(n):
                    last = nc.scalar.activation(y[par][0:rows, s, :], y[par][0:rows, s, :], ACT.Copy, scale=factor[par][0:rows, s:s + 1])
                last.then_inc(gated, 1)
                act.wait_ge(mixed, n + 1)
                if not is_last(n):
                    act.dma_start(group(outfull, n), xr[par][:, :, :]).then_inc(stored[par], 16)
                else:
                    for s, rows in row_tiles(n):
                        at = n * GROUP + s * P
                        act.dma_start(out[at:at + rows, :], xr[par][0:rows, s, :]).then_inc(stored[par], 16)

            over_steps(act, step)
            act.wait_ge(stored[0], 16 * (NT // 2 + len(row_tiles(LAST))))
            act.wait_ge(stored[1], 16 * (NT // 2))

        @block.vector
        def _(dve):
            def stage(n, par):
                c = len(row_tiles(n))
                for s0, c, rows in row_parts(n):
                    nc.vector.tensor_copy(factor[par][0:rows, s0:s0 + c], gate[0:rows, bass.ds(n * 4 + s0, c)])
                    last = nc.vector.tensor_copy(index[par][0:rows, s0:s0 + c], gidx[0:rows, bass.ds(n * 4 + s0, c)])
                last.then_inc(staged, 1)

            def step(n, par):
                parts = row_parts(n)
                dve.wait_ge(gated, n + 1)
                for s0, c, rows in parts:
                    v = slice(0, rows), slice(s0, s0 + c), slice(None)
                    nc.vector.tensor_scalar(odd[v], y[par][v], 0.0, 0.0, ALU.mult, ALU.not_equal)
                    nc.vector.tensor_scalar(above[v], y[par][v], 0.0, 1e4, ALU.max, ALU.min)
                    last = nc.vector.tensor_scalar(below[v], y[par][v], 0.0, -1e4, ALU.min, ALU.max)
                last.then_inc(split, 1)
                dve.wait_ge(split, n + 1)
                for s0, c, rows in parts:
                    v = slice(0, rows), slice(s0, s0 + c), slice(None)
                    last = nc.vector.tensor_tensor(above[v], above[v], below[v], ALU.add)
                last.then_inc(joined, 1)
                after(dve, joined, n + 1, held)
                for s0, c, rows in parts:
                    v = slice(0, rows), slice(s0, s0 + c), slice(None)
                    last = nc.vector.copy_predicated(y[par][v], odd[v].bitcast(I32), above[v])
                last.then_inc(cleaned, 1)
                dve.wait_ge(x_in[par], (uses(n, par) - 1 + (len(row_tiles(n)) if is_last(n) else 1)) * 16)
                dve.wait_ge(cleaned, n + 1)
                for s0, c, rows in parts:
                    v = slice(0, rows), slice(s0, s0 + c), slice(None)
                    last = nc.vector.tensor_tensor(xr[par][v], xr[par][v], y[par][v], ALU.add)
                last.then_inc(mixed, 1)
                if not static(n) or n + 2 <= LAST:
                    after(dve, mixed, n + 1, held)
                    stage(n + 2, par)

            stage(0, 0)
            stage(1, 1)
            step(0, 0)
            step(1, 1)
            with dve.Fori(1, NT // 2 - 1) as i:
                step(i * 2, 0)
                step(i * 2 + 1, 1)
            for n in range(2 * (NT // 2 - 1), NT):
                step(n, n % 2)


_INS = ["x", "src", "dst", "L0_gnn_eps", "L0_gnn_W1", "L0_gnn_b1", "L0_gnn_g1", "L0_gnn_beta1", "L0_gnn_W2", "L0_gnn_b2",
        "L0_gnn_g2", "L0_gnn_beta2", "L0_gnn_W3", "L0_gnn_b3", "L0_gnn_g3", "L0_gnn_beta3", "L0_gnn_W4", "L0_gnn_b4",
        "L0_ffn_gate_w", "L0_ffn_gate_b", "L0_ffn_w1", "L0_ffn_b1", "L0_ffn_w2", "L0_ffn_b2"]


def kernel(**inputs):
    import numpy as np
    import concourse.bacc as bacc
    from concourse import mybir as mb
    from concourse.bass_utils import run_bass_kernel_spmd

    nc = bacc.Bacc("TRN2", target_bir_lowering=False, num_devices=1)
    arrays, args = {}, {}
    for name in _INS:
        v = np.ascontiguousarray(inputs[name])
        arrays[f"in_{name}_dram"] = v
        args[name] = nc.dram_tensor(f"in_{name}_dram", v.shape, mb.dt.from_np(v.dtype), kind="ExternalInput").ap()
    out = nc.dram_tensor("out_0_dram", (N, D), mb.dt.float32, kind="ExternalOutput").ap()
    gnn_ffn_program(nc, args, out)
    r = run_bass_kernel_spmd(nc, [arrays], core_ids=[0])
    return r.results[0]["out_0_dram"]
```

```python
import concourse.bass as bass
from concourse import mybir
from contextlib import ExitStack

F32 = mybir.dt.float32
F32R = mybir.dt.float32r
I32 = mybir.dt.int32
I16 = mybir.dt.int16
ALU = mybir.AluOpType
ACT = mybir.ActivationFunctionType
AX = mybir.AxisListType

P = 128
N, D = 12500, 256
E = 200000
CH = [256, 512, 1024, 512, 256]
LN_EPS = BN_EPS = 1e-5

GROUP = 4 * P
NG = -(-N // GROUP)
NTILES = -(-N // P)
NPAD = NTILES * P
TILE = 500
NT = N // TILE
assert NT == NG and NT % 2 == 1 and NT * TILE == N
LAST = NT - 1
TAIL = N - LAST * GROUP

CPB = 4
EB = CPB * P
BODY = 8
SLOTS = 4
NBLK = -(-E // (EB * BODY)) * BODY
BQ = 4
BP = NBLK // BQ
assert BP * BQ == NBLK and BP <= P

NE, F = 8, 1024
CAP = -(-(5 * N) // (4 * NE))
XT = [GROUP, GROUP, GROUP, CAP - 3 * GROUP]
BUFROWS = -(-(NE * CAP + 2 * GROUP) // P) * P
NUMBER = 2 * D + NE
ROW = -(-(NUMBER + 1) // 16) * 16
RING = 4
FAR = 1 << 20

VECS = [("L0_gnn_b1", 4), ("L0_gnn_g1", 4), ("L0_gnn_beta1", 4),
        ("L0_gnn_b2", 8), ("L0_gnn_g2", 8), ("L0_gnn_beta2", 8),
        ("L0_gnn_b3", 4), ("L0_gnn_g3", 4), ("L0_gnn_beta3", 4)]
VCOL, _at = {}, 0
for _n, _c in VECS:
    VCOL[_n] = _at
    _at += _c
NVEC = _at
NB1 = NE * F // P


def row_parts(n):
    if not is_last(n):
        return [(0, 4, P)]
    full, rest = divmod(TAIL, P)
    return [(0, full, P), (full, 1, rest)]


def row_tiles(n):
    return [(s, rows) for a, c, rows in row_parts(n) for s in range(a, a + c)]


def static(n):
    return isinstance(n, int)


def is_last(n):
    return static(n) and n == LAST


def over_steps(eng, step):
    step(0, 0)
    step(1, 1)
    with eng.Fori(1, NT // 2) as i:
        step(i * 2, 0)
        step(i * 2 + 1, 1)
    step(LAST, LAST % 2)


def uses(n, par):
    return n // 2 + 1 if static(n) else (n - par) // 2 + 1


def after(eng, sem, value, held):
    eng.wait_ge(sem, value)
    eng.sem_inc(held, 1)


def gnn_ffn_program(nc, a, out):
    def dram(name, shape, dt=F32):
        return nc.dram_tensor(name, shape, dt, kind="Internal").ap()

    xln_d = dram("xln_d", [N, D])
    range_d = dram("range_d", [NBLK, 2], I32)
    h_d = [dram(f"h{k}_d", [CH[k], N]) for k in (1, 2, 3)]
    buf_d = dram("buf_d", [BUFROWS, ROW])

    whole = ExitStack()
    with whole:
        def outer(name, shape, dt=F32, scope=whole):
            return scope.enter_context(nc.sbuf_tensor(name, shape, dt))

        ident = outer("ident", [P, P])
        vec = outer("vec", [P, NVEC])
        b1e = outer("b1e", [P, NB1])
        epsln = outer("epsln", [P, 1])
        stats = outer("stats", [P, 8, NT, 6])

        mid = ExitStack()
        with mid:
            w2h = outer("w2h", [P, 4, CH[2]], F32R, mid)
            w2l = outer("w2l", [P, 4, CH[2]], F32R, mid)
            first = ExitStack()
            with first:
                acc = outer("acc", [P, 2, NPAD], F32, first)
                w1h = outer("w1h", [P, 2, CH[1]], F32R, first)
                w1l = outer("w1l", [P, 2, CH[1]], F32R, first)
                edges = ExitStack()
                with edges:
                    src_t = outer("src_t", [P, NBLK * CPB], I32, edges)
                    ndst_t = outer("ndst_t", [P, NBLK * CPB], F32, edges)
                    trow = outer("trow", [1, NBLK * 2], I32, edges)
                    prepare(nc, a, xln_d, range_d, ident, vec, b1e, epsln, w1h, w1l,
                            acc, src_t, ndst_t, trow)
                    aggregate(nc, xln_d, buf_d, acc, src_t, ndst_t, trow)
                layer(nc, 1, a, None, h_d[0], acc, stats, vec, epsln, (w1h, w1l),
                      (a["L0_gnn_W2"], w2h, w2l))
            w3h = outer("w3h", [P, 8, CH[3]], F32R, mid)
            w3l = outer("w3l", [P, 8, CH[3]], F32R, mid)
            layer(nc, 2, a, h_d[0], h_d[1], None, stats, vec, epsln, (w2h, w2l),
                  (a["L0_gnn_W3"], w3h, w3l))
            layer(nc, 3, a, h_d[1], h_d[2], None, stats, vec, epsln, (w3h, w3l), None)
        ew = {name: outer(f"e_{name}", shape) for name, shape in (("w1raw", [P, D // P, F]), ("w2raw", [P, F // P, D]))}
        for name, shape, dt in (("w1h", [P, D // P, F], F32R), ("w1l", [P, D // P, F], F32R),
                                ("w2h", [P, F // P, D], F32R), ("w2l", [P, F // P, D], F32R), ("b2", [P, 1, D], F32)):
            ew[name] = [outer(f"e_{name}{k}", shape, dt) for k in range(2)]
        last_layer(nc, a, out, h_d[2], buf_d, stats, vec, epsln, ident, ew)
        experts(nc, a, buf_d, out, ident, b1e, ew)


def prepare(nc, a, xln_d, range_d, ident, vec, b1e, epsln, w1h, w1l,
            acc, src_t, ndst_t, trow):
    ctx = ExitStack()
    with ctx:
        def sb(name, shape, dt=F32):
            return ctx.enter_context(nc.sbuf_tensor("a_" + name, shape, dt))

        sems = []

        def sem(name):
            sems.append(nc.alloc_semaphore("a_" + name))
            return sems[-1]

        src_raw = sb("src_raw", [BP, BQ, EB], I32)
        dst_raw = sb("dst_raw", [BP, BQ, EB], I32)
        src_f, dst_f = src_raw[:, :, :].bitcast(F32), dst_raw[:, :, :].bitcast(F32)
        reach_f = sb("reach_f", [BP, BQ, 2])
        reach = sb("reach", [BP, BQ, 2], I32)
        vraw = sb("vraw", [NVEC, P])
        b1raw = sb("b1raw", [NB1, P])
        ope = sb("ope", [P, 1])
        w1raw = sb("w1raw", [P, 2, CH[1]])
        xg = [sb(f"xg{k}", [P, 4, D]) for k in range(2)]
        xn = [sb(f"xn{k}", [P, 4, D]) for k in range(2)]
        st = [sb(f"st{k}", [P, 4, 6]) for k in range(2)]
        mv = [sb(f"mv{k}", [P, 4, 2]) for k in range(2)]
        rs = [sb(f"rs{k}", [P, 4]) for k in range(2)]
        ps_x = [ctx.enter_context(nc.psum_tensor(f"a_ps_x{k}", [P, 2, GROUP], F32)) for k in range(2)]
        ps_e = [ctx.enter_context(nc.psum_tensor(f"a_ps_e{k}", [P, 512], F32)) for k in range(4)]

        pads, const, held = sem("pads"), sem("const"), sem("held")
        edges_in, vec_in, eps_in, w_in = sem("edges_in"), sem("vec_in"), sem("eps_in"), sem("w_in")
        x_in = [sem(f"x_in{k}") for k in range(2)]
        cast, reached, shifted, range_out, range_in = (sem("cast"), sem("reached"), sem("shifted"),
                                                       sem("range_out"), sem("range_in"))
        src_turned, dst_turned, src_kept, dst_kept = (sem("src_turned"), sem("dst_turned"),
                                                      sem("src_kept"), sem("dst_kept"))
        vec_turned, vec_kept, scaled = sem("vec_turned"), sem("vec_kept"), sem("scaled")
        w_high, w_low = sem("w_high"), sem("w_low")
        summed, moments, rooted, inverse, normed = (sem("summed"), sem("moments"), sem("rooted"),
                                                    sem("inverse"), sem("normed"))
        turned, kept = sem("turned"), sem("kept")
        xln_out = [sem(f"xln_out{k}") for k in range(2)]
        EDGE_LOADS = 6

        ctx.callback(nc.all_engine_barrier)
        ctx.callback(nc.clear_and_free_semaphores, sems)
        xfull = a["x"][0:LAST * GROUP, :].rearrange("(g s p) f -> g p s f", s=4, p=P)
        nfull = xln_d[0:LAST * GROUP, :].rearrange("(g s p) f -> g p s f", s=4, p=P)

        def group(view, n):
            if static(n):
                return view[n]
            return view[bass.ds(n, 1)].rearrange("o p s f -> (o p) s f")

        block = ctx.enter_context(nc.Block())

        @block.sync
        def _(sp):
            def load(n, par):
                if not is_last(n):
                    if not static(n):
                        sp.wait_ge(normed, n - 1)
                    sp.dma_start(xg[par][:, :, :], group(xfull, n)).then_inc(x_in[par], 16)
                else:
                    sp.wait_ge(normed, n - 1)
                    for s, rows in row_tiles(n):
                        at = n * GROUP + s * P
                        sp.dma_start(xg[par][0:rows, s, :], a["x"][at:at + rows, :]).then_inc(x_in[par], 16)

            sp.wait_ge(pads, 2)
            whole_blocks, rest = divmod(E, EB)
            low = (BQ - 1) * BP
            for raw, name in ((src_raw, "src"), (dst_raw, "dst")):
                sp.dma_start(raw[:, 0:BQ - 1, :],
                             a[name][0:low * EB].rearrange("(q p e) -> p q e", q=BQ - 1, e=EB)).then_inc(edges_in, 16)
                sp.dma_start(raw[0:whole_blocks - low, BQ - 1, :],
                             a[name][low * EB:whole_blocks * EB].rearrange("(p e) -> p e", e=EB)).then_inc(edges_in, 16)
                sp.dma_start(raw[whole_blocks - low:whole_blocks - low + 1, BQ - 1, 0:rest],
                             a[name][whole_blocks * EB:E].rearrange("(p e) -> p e", p=1)).then_inc(edges_in, 16)
            over_steps(sp, load)
            sp.wait_ge(shifted, 4)
            sp.dma_start(range_d.rearrange("(q p) c -> p q c", q=BQ), reach[:, :, :]).then_inc(range_out, 16)
            sp.wait_ge(range_out, 16)
            sp.dma_start(trow[:, :], range_d.rearrange("(o b) c -> o (b c)", o=1)).then_inc(range_in, 16)
            sp.wait_ge(range_in, 16)

        @block.gpsimd
        def _(pool):
            nc.gpsimd.memset(src_raw[:, BQ - 1, :], 0).then_inc(pads, 1)
            nc.gpsimd.memset(dst_raw[:, BQ - 1, :], NPAD - 1).then_inc(pads, 1)
            nc.gpsimd.memset(epsln[:, :], LN_EPS).then_inc(const, 1)
            nc.gpsimd.memset(ident[:, :], 0.0).then_inc(const, 1)
            nc.gpsimd.memset(acc[:, :, N:NPAD], 0.0).then_inc(const, 1)
            pool.wait_ge(const, 3)
            nc.gpsimd.affine_select(out=ident[:, :], in_=ident[:, :], compare_op=ALU.not_equal, fill=1.0,
                                    base=0, pattern=[[-1, P]], channel_multiplier=1).then_inc(const, 1)

            def store(n, par):
                if not is_last(n):
                    after(pool, normed, n + 1, held)
                    pool.dma_start(group(nfull, n), xn[par][:, :, :]).then_inc(xln_out[par], 16)
                else:
                    pool.wait_ge(normed, n + 1)
                    for s, rows in row_tiles(n):
                        at = n * GROUP + s * P
                        pool.dma_start(xln_d[at:at + rows, :], xn[par][0:rows, s, :]).then_inc(xln_out[par], 16)

            over_steps(pool, store)
            pool.wait_ge(xln_out[0], 16 * (NT // 2 + len(row_tiles(LAST))))
            pool.wait_ge(xln_out[1], 16 * (NT // 2))

        @block.scalar
        def _(act):
            at = 0
            for name, c in VECS:
                act.dma_start(vraw[at:at + c, :], a[name].rearrange("(c p) -> c p", p=P)).then_inc(vec_in, 16)
                at += c
            act.dma_start(b1raw[:, :], a["L0_ffn_b1"].rearrange("e (c p) -> (e c) p", p=P)).then_inc(vec_in, 16)
            act.dma_start(ope[:, :], a["L0_gnn_eps"].rearrange("(o c) -> o c", o=1).to_broadcast([P, 1])).then_inc(eps_in, 16)
            act.dma_start(w1raw[:, :, :], a["L0_gnn_W1"].rearrange("(c p) m -> p c m", p=P)).then_inc(w_in, 16)
            act.wait_ge(w_in, 16)
            nc.scalar.copy(w1h[:, :, :], w1raw[:, :, :]).then_inc(w_high, 1)
            dview = ndst_t[:, :].rearrange("p (b j) -> p b j", j=CPB)
            for j in range(CPB):
                act.wait_ge(dst_turned, j + 1)
                nc.scalar.mul(dview[:, :, j], ps_e[j][:, 0:NBLK], -1.0).then_inc(dst_kept, 1)
            act.wait_ge(scaled, 1)

            def step(n, par):
                act.wait_ge(moments, n + 1)
                for s0, c, rows in row_parts(n):
                    last = nc.scalar.activation(rs[par][0:rows, s0:s0 + c], mv[par][0:rows, s0:s0 + c, 1], ACT.Sqrt,
                                                bias=epsln[0:rows, 0:1])
                last.then_inc(rooted, 1)
                cols = TAIL if is_last(n) else GROUP
                after(act, turned, n + 1, held)
                nc.scalar.activation(acc[:, :, bass.ds(n * GROUP, cols)], ps_x[par][:, :, 0:cols], ACT.Copy,
                                     scale=ope[:, 0:1]).then_inc(kept, 1)

            over_steps(act, step)

        @block.vector
        def _(dve):
            dve.wait_ge(edges_in, 16 * EDGE_LOADS)
            nc.vector.tensor_scalar(src_f[:, :, :], src_raw[:, :, :], 0.0, float(N - 1), ALU.max, ALU.min).then_inc(cast, 1)
            nc.vector.tensor_copy(dst_f[:, :, :], dst_raw[:, :, :]).then_inc(cast, 1)
            dve.wait_ge(cast, 2)
            nc.vector.tensor_reduce(reach_f[:, :, 0], dst_f[:, :, :], AX.X, ALU.min).then_inc(reached, 1)
            nc.vector.tensor_reduce(reach_f[:, :, 1], dst_f[:, :, :], AX.X, ALU.max).then_inc(reached, 1)
            dve.wait_ge(reached, 2)
            nc.vector.tensor_copy(reach[:, :, :], reach_f[:, :, :]).then_inc(shifted, 1)
            dve.wait_ge(shifted, 1)
            nc.vector.tensor_scalar(reach[:, :, :], reach[:, :, :], P.bit_length() - 1, None, ALU.arith_shift_right).then_inc(shifted, 1)
            dve.wait_ge(shifted, 2)
            nc.vector.tensor_scalar(reach[:, :, :], reach[:, :, :], 0.0, float(NTILES - 1), ALU.max, ALU.min).then_inc(shifted, 1)
            dve.wait_ge(shifted, 3)
            nc.vector.tensor_scalar(reach[:, :, 1], reach[:, :, 1], 1.0, None, ALU.add).then_inc(shifted, 1)
            dve.wait_ge(eps_in, 16)
            nc.vector.tensor_scalar(ope[:, :], ope[:, :], 1.0, None, ALU.add).then_inc(scaled, 1)
            sview = src_t[:, :].rearrange("p (b j) -> p b j", j=CPB)
            for j in range(CPB):
                dve.wait_ge(src_turned, j + 1)
                nc.vector.tensor_copy(sview[:, :, j], ps_e[j][:, 0:NBLK]).then_inc(src_kept, 1)
            dve.wait_ge(vec_turned, 1)
            nc.vector.tensor_copy(vec[:, :], ps_x[0][:, 0, 0:NVEC]).then_inc(vec_kept, 1)
            nc.vector.tensor_copy(b1e[:, :], ps_x[1][:, 0, 0:NB1]).then_inc(vec_kept, 1)

            def step(n, par):
                loads = len(row_tiles(n)) if is_last(n) else 1
                for s, rows in row_tiles(n):
                    if s == 0:
                        dve.wait_ge(x_in[par], (uses(n, par) - 1 + loads) * 16)
                    last = nc.vector.bn_stats(st[par][0:rows, s, :], xg[par][0:rows, s, :])
                last.then_inc(summed, 1)
                after(dve, summed, n + 1, held)
                for s, rows in row_tiles(n):
                    last = nc.vector.bn_aggr(mv[par][0:rows, s, :], st[par][0:rows, s, :])
                last.then_inc(moments, 1)
                dve.wait_ge(rooted, n + 1)
                for s0, c, rows in row_parts(n):
                    last = nc.vector.reciprocal(rs[par][0:rows, s0:s0 + c], rs[par][0:rows, s0:s0 + c])
                last.then_inc(inverse, 1)
                if not static(n) or n >= 2:
                    dve.wait_ge(turned, n - 1)
                    dve.wait_ge(xln_out[par], (uses(n, par) - 1) * 16)
                dve.wait_ge(inverse, n + 1)
                for s, rows in row_tiles(n):
                    last = nc.vector.tensor_scalar(xn[par][0:rows, s, :], xg[par][0:rows, s, :], mv[par][0:rows, s, 0:1],
                                                   rs[par][0:rows, s:s + 1], ALU.subtract, ALU.mult)
                last.then_inc(normed, 1)

            over_steps(dve, step)
            dve.wait_ge(w_high, 1)
            nc.vector.tensor_tensor(w1l[:, :, :], w1raw[:, :, :], w1h[:, :, :].bitcast(F32), ALU.subtract).then_inc(w_low, 1)

        @block.tensor
        def _(pe):
            pe.wait_ge(const, 4)
            pe.wait_ge(cast, 2)
            for j in range(CPB):
                for q in range(BQ):
                    last = pe.transpose(ps_e[j][:, q * BP:(q + 1) * BP], src_f[:, q, j * P:(j + 1) * P], ident[0:BP, 0:BP])
                last.then_inc(src_turned, 1)
            for j in range(CPB):
                pe.wait_ge(src_kept, j + 1)
                for q in range(BQ):
                    last = pe.transpose(ps_e[j][:, q * BP:(q + 1) * BP], dst_f[:, q, j * P:(j + 1) * P], ident[0:BP, 0:BP])
                last.then_inc(dst_turned, 1)
            pe.wait_ge(vec_in, 16 * (len(VECS) + 1))
            pe.transpose(ps_x[0][:, 0, 0:NVEC], vraw[:, :], ident[0:NVEC, 0:NVEC])
            pe.transpose(ps_x[1][:, 0, 0:NB1], b1raw[:, :], ident[0:NB1, 0:NB1]).then_inc(vec_turned, 1)
            pe.wait_ge(vec_kept, 2)

            def step(n, par):
                if not static(n) or n >= 2:
                    pe.wait_ge(kept, n - 1)
                pe.wait_ge(normed, n + 1)
                for h in range(2):
                    for s, rows in row_tiles(n):
                        last = pe.transpose(ps_x[par][:, h, s * P:s * P + rows], xn[par][0:rows, s, h * P:(h + 1) * P],
                                            ident[0:rows, 0:rows])
                last.then_inc(turned, 1)

            over_steps(pe, step)


def aggregate(nc, xln_d, buf_d, acc, src_t, ndst_t, trow):
    ctx = ExitStack()
    with ctx:
        def sb(name, shape, dt=F32):
            return ctx.enter_context(nc.sbuf_tensor("b_" + name, shape, dt))

        def sem(name):
            return ctx.enter_context(nc.semaphore("b_" + name))

        HALF = BODY // 2
        rows = sb("rows", [P, SLOTS, CPB, D])
        index = [sb(f"index{k}", [P, HALF * CPB], I32) for k in range(2)]
        nodes = sb("nodes", [P, NPAD], I16)
        away = sb("away", [P, EB])
        onehot = sb("onehot", [P, 2 * EB])
        one = sb("one", [P, 1])
        empty = sb("empty", [P, 1, ROW])
        ps = ctx.enter_context(nc.psum_tensor("b_ps", [P, 2 * 512], F32))

        const, held, zeroed = sem("const"), sem("held"), sem("zeroed")
        indexed = [sem(f"indexed{k}") for k in range(2)]
        gathered = [sem(f"gathered{k}") for k in range(SLOTS)]
        slot_free, product, added = sem("slot_free"), sem("product"), sem("added")
        apart, picked = sem("apart"), sem("picked")
        block = ctx.enter_context(nc.Block())

        def bounds(eng, i, name):
            regs = [eng.alloc_register(f"{name}{q}") for q in range(2 * BODY)]
            eng.load(regs, trow[0:1, bass.ds(i * (2 * BODY), 2 * BODY)])
            return [eng.snap(r, min_val=0, max_val=NTILES) for r in regs]

        @block.sync
        def _(sp):
            sp.wait_ge(const, 5)
            sp.dma_start(buf_d.rearrange("(p r) f -> p r f", p=P),
                         empty[:, :, :].to_broadcast([P, BUFROWS // P, ROW])).then_inc(zeroed, 16)

            def stage(i, k):
                sp.dma_start(index[k][:, :], src_t[:, bass.ds((i * BODY + k * HALF) * CPB, HALF * CPB)]).then_inc(indexed[k], 16)

            stage(0, 0)
            stage(0, 1)
            with sp.Fori(1, NBLK // BODY) as i:
                for k in range(2):
                    sp.wait_ge(slot_free, SLOTS + i * BODY - BODY + (k + 1) * HALF)
                    stage(i, k)
            sp.wait_ge(zeroed, 16)

        @block.gpsimd
        def _(pool):
            nc.gpsimd.memset(empty[:, :, :], 0.0).then_inc(const, 1)
            nc.gpsimd.memset(one[:, :], 1.0).then_inc(const, 1)
            nc.gpsimd.iota(nodes[:, :], pattern=[[1, NPAD]], base=0, channel_multiplier=0).then_inc(const, 1)
            nc.gpsimd.memset(away[:, 0:1], 0.0).then_inc(const, 1)
            pool.wait_ge(const, 4)
            nc.gpsimd.memset(empty[:, :, NUMBER:NUMBER + 1].bitcast(I32), FAR).then_inc(const, 1)
            with pool.Fori(0, NBLK // BODY) as i:
                for k in range(BODY):
                    if k % HALF == 0:
                        after(pool, indexed[k // HALF], i * 16 + 16, held)
                    after(pool, slot_free, i * BODY + k + 1, held)
                    for j in range(CPB):
                        at = (k % HALF) * CPB + j
                        pool.indirect_dma_start(rows[:, k % SLOTS, j, :], None, xln_d,
                                                bass.IndirectOffsetOnAxis(index[k // HALF][:, at:at + 1], 0)
                                                ).then_inc(gathered[k % SLOTS], 16)

        @block.scalar
        def _(act):
            act.wait_ge(const, 5)
            act.sem_inc(picked, 1)
            step = act.alloc_register("act_step")
            act.reg_mov(step, 0)
            with act.Fori(0, NBLK // BODY) as i:
                r = bounds(act, i, "act_b")
                for k in range(BODY):
                    with act.Fori(r[2 * k], r[2 * k + 1]) as t:
                        s = act.snap(step)
                        ring = act.snap((s % 2) * EB)
                        after(act, product, s + 1, held)
                        after(act, picked, s + 1, held)
                        for j in range(CPB):
                            last = nc.scalar.activation(away[:, j * P:(j + 1) * P], nodes[:, bass.ds(t * P, P)], ACT.Abs,
                                                        bias=ndst_t[:, bass.ds((i * BODY + k) * CPB + j, 1)])
                        last.then_inc(apart, 1)
                        after(act, apart, s + 1, held)
                        nc.scalar.activation(onehot[:, bass.ds(ring, EB)], away[:, :], ACT.Relu,
                                             scale=-1.0, bias=one[:, 0:1]).then_inc(picked, 1)
                        act.reg_add(step, step, 1)

        @block.tensor
        def _(pe):
            pe.sem_inc(slot_free, SLOTS)
            pe.sem_inc(product, 2)
            step = pe.alloc_register("pe_step")
            pe.reg_mov(step, 0)
            with pe.Fori(0, NBLK // BODY) as i:
                r = bounds(pe, i, "pe_b")
                for k in range(BODY):
                    after(pe, gathered[k % SLOTS], (i * (BODY // SLOTS) + k // SLOTS + 1) * (CPB * 16), held)
                    with pe.Fori(r[2 * k], r[2 * k + 1]):
                        s = pe.snap(step)
                        ring = pe.snap((s % 2) * 512)
                        after(pe, added, s + 1, held)
                        after(pe, picked, s + 2, held)
                        for h in range(2):
                            for j in range(CPB):
                                last = pe.matmul(ps[:, bass.ds(ring + h * P, P)], rows[:, k % SLOTS, j, h * P:(h + 1) * P],
                                                 onehot[:, bass.ds(ring + j * P, P)], start=(j == 0), stop=(j == CPB - 1))
                        last.then_inc(product, 1)
                        pe.reg_add(step, step, 1)
                    pe.drain().then_inc(slot_free, 1)

        @block.vector
        def _(dve):
            dve.sem_inc(added, 2)
            step = dve.alloc_register("dve_step")
            dve.reg_mov(step, 0)
            with dve.Fori(0, NBLK // BODY) as i:
                r = bounds(dve, i, "dve_b")
                for k in range(BODY):
                    with dve.Fori(r[2 * k], r[2 * k + 1]) as t:
                        s = dve.snap(step)
                        ring = dve.snap((s % 2) * 512)
                        after(dve, added, s + 2, held)
                        after(dve, product, s + 3, held)
                        nc.vector.tensor_tensor(acc[:, :, bass.ds(t * P, P)],
                                                ps[:, bass.ds(ring, 2 * P)].rearrange("p (h n) -> p h n", h=2),
                                                acc[:, :, bass.ds(t * P, P)], ALU.add).then_inc(added, 1)
                        dve.reg_add(step, step, 1)




def layer(nc, which, a, h_in, h_out, acc, stats, vec, epsln, w, nextw):
    K, M = CH[which - 1] // P, CH[which] // P
    normal = which > 1
    ctx = ExitStack()
    with ctx:
        tag = f"l{which}_"

        def sb(name, shape, dt=F32):
            return ctx.enter_context(nc.sbuf_tensor(tag + name, shape, dt))

        def sem(name):
            return ctx.enter_context(nc.semaphore(tag + name))

        bias_at = VCOL[f"L0_gnn_b{which}"]
        if normal:
            g_at, beta_at = VCOL[f"L0_gnn_g{which - 1}"], VCOL[f"L0_gnn_beta{which - 1}"]
            hin = [sb(f"hin{k}", [P, K, TILE]) for k in range(2)]
            ex = sb("ex", [P, K, TILE])
            mv = sb("mv", [P, K, 2])
            scale = sb("scale", [P, K])
            shift = sb("shift", [P, K])
            hin_v = h_in.rearrange("(m p) n -> p m n", p=P)
        zh = [sb(f"zh{k}", [P, K, TILE], F32R) for k in range(2)]
        zl = [sb(f"zl{k}", [P, K, TILE], F32R) for k in range(2)]
        hout = [sb(f"hout{k}", [P, M, TILE]) for k in range(2)]
        hout_v = h_out.rearrange("(m p) n -> p m n", p=P)
        ps = [ctx.enter_context(nc.psum_tensor(f"{tag}ps{k}", [P, 512], F32)) for k in range(8)]
        if nextw:
            nraw = sb("nraw", list(nextw[1].shape))

        held, bn_done, bn_root, bn_ready = sem("held"), sem("bn_done"), sem("bn_root"), sem("bn_ready")
        next_in, next_split = sem("next_in"), sem("next_split")
        loaded = [sem(f"loaded{k}") for k in range(2)]
        exped, bounded, active, high, low = sem("exped"), sem("bounded"), sem("active"), sem("high"), sem("low")
        product, biased, counted = sem("product"), sem("biased"), sem("counted")
        stored = [sem(f"stored{k}") for k in range(2)]
        block = ctx.enter_context(nc.Block())
        HALVES = [slice(0, K // 2), slice(K // 2, K)]

        @block.sync
        def _(sp):
            if normal:
                def load(n, par):
                    if not static(n) or n >= 2:
                        sp.wait_ge(low, n * 2 - 2)
                    sp.dma_start(hin[par][:, :, :], hin_v[:, :, bass.ds(n * TILE, TILE)]).then_inc(loaded[par], 16)

                over_steps(sp, load)

        @block.gpsimd
        def _(pool):
            def store(n, par):
                after(pool, biased, n * M + M, held)
                pool.dma_start(hout_v[:, :, bass.ds(n * TILE, TILE)], hout[par][:, :, :]).then_inc(stored[par], 16)

            if nextw:
                pool.dma_start(nraw[:, :, :], nextw[0].rearrange("(c p) m -> p c m", p=P)).then_inc(next_in, 16)
                pool.wait_ge(next_in, 16)
                nc.gpsimd.tensor_copy(nextw[1][:, :, :], nraw[:, :, :]).then_inc(next_split, 1)
                pool.wait_ge(next_split, 1)
                nc.gpsimd.tensor_tensor(nextw[2][:, :, :], nraw[:, :, :], nextw[1][:, :, :].bitcast(F32),
                                        ALU.subtract).then_inc(next_split, 1)
            over_steps(pool, store)
            pool.wait_ge(stored[0], 16 * (NT // 2 + 1))
            pool.wait_ge(stored[1], 16 * (NT // 2))

        @block.scalar
        def _(act):
            if normal:
                act.wait_ge(bn_done, 1)
                nc.scalar.activation(scale[:, :], mv[:, :, 1], ACT.Sqrt, bias=epsln[:, 0:1]).then_inc(bn_root, 1)
                act.wait_ge(bn_ready, 3)

            def prep(n, par):
                for k, half in enumerate(HALVES):
                    if not static(n) or n >= 1:
                        act.wait_ge(active, n * 2 + k - 1)
                    if k == 0:
                        act.wait_ge(loaded[par], uses(n, par) * 16)
                    for c in range(half.start, half.stop):
                        nc.scalar.activation(ex[:, c, :], hin[par][:, c, :], ACT.Exp, bias=shift[:, c:c + 1], scale=scale[:, c:c + 1])
                        last = nc.scalar.activation(hin[par][:, c, :], hin[par][:, c, :], ACT.Identity, bias=shift[:, c:c + 1],
                                                    scale=scale[:, c:c + 1])
                    last.then_inc(exped, 1)

            def finish(n, par):
                if not static(n) or n >= 2:
                    act.wait_ge(stored[par], (uses(n, par) - 1) * 16)
                    act.wait_ge(counted, n - 1)
                for m in range(M):
                    act.wait_ge(product, n * M + m + 1)
                    nc.scalar.activation(hout[par][:, m, :], ps[(par * M + m) % 8][:, 0:TILE], ACT.Identity,
                                         bias=vec[:, bias_at + m:bias_at + m + 1]).then_inc(biased, 1)

            def step(n, par):
                if normal and not is_last(n):
                    prep(n + 1, 1 - par)
                finish(n, par)

            if normal:
                prep(0, 0)
            over_steps(act, step)

        @block.vector
        def _(dve):
            if normal:
                for c in range(K):
                    last = nc.vector.bn_aggr(mv[:, c, :], stats[:, c, :, :].rearrange("p t s -> p (t s)"))
                last.then_inc(bn_done, 1)
                dve.wait_ge(bn_root, 1)
                nc.vector.reciprocal(scale[:, :], scale[:, :]).then_inc(bn_ready, 1)
                dve.wait_ge(bn_ready, 1)
                nc.vector.tensor_tensor(scale[:, :], scale[:, :], vec[:, g_at:g_at + K], ALU.mult).then_inc(bn_ready, 1)
                dve.wait_ge(bn_ready, 2)
                nc.vector.tensor_tensor(shift[:, :], scale[:, :], mv[:, :, 0], ALU.mult).then_inc(bn_done, 1)
                dve.wait_ge(bn_done, 2)
                nc.vector.tensor_tensor(shift[:, :], vec[:, beta_at:beta_at + K], shift[:, :], ALU.subtract).then_inc(bn_ready, 1)

            def prep(n, par):
                for k, half in enumerate(HALVES):
                    if normal:
                        dve.wait_ge(exped, n * 2 + k + 1)
                        nc.vector.tensor_scalar(ex[:, half, :], ex[:, half, :], 1.0, 0.0, ALU.subtract, ALU.min).then_inc(bounded, 1)
                        dve.wait_ge(bounded, n * 2 + k + 1)
                        nc.vector.tensor_tensor(hin[par][:, half, :], hin[par][:, half, :], ex[:, half, :], ALU.max).then_inc(active, 1)
                        z = hin[par][:, half, :]
                        dve.wait_ge(active, n * 2 + k + 1)
                    else:
                        z = acc[:, half, bass.ds(n * TILE, TILE)]
                    if k == 0 and (not static(n) or n >= 2):
                        after(dve, product, n * M - M, held)
                    nc.vector.tensor_copy(zh[par][:, half, :], z).then_inc(high, 1)
                    dve.wait_ge(high, n * 2 + k + 1)
                    nc.vector.tensor_tensor(zl[par][:, half, :], z, zh[par][:, half, :].bitcast(F32), ALU.subtract).then_inc(low, 1)

            def finish(n, par):
                after(dve, biased, n * M + M, held)
                for m in range(M):
                    last = nc.vector.bn_stats(stats[:, m, bass.ds(n, 1), :].rearrange("p o s -> p (o s)"), hout[par][:, m, :])
                last.then_inc(counted, 1)

            def step(n, par):
                if not is_last(n):
                    prep(n + 1, 1 - par)
                finish(n, par)

            prep(0, 0)
            over_steps(dve, step)

        @block.tensor
        def _(pe):
            def step(n, par):
                for m in range(M):
                    if not static(n) or n * M + m >= 8:
                        pe.wait_ge(biased, n * M + (m + 1 - 8))
                    o = ps[(par * M + m) % 8][:, 0:TILE]
                    cols = slice(m * P, (m + 1) * P)
                    for c in range(K):
                        if m == 0 and c in (0, K // 2):
                            pe.wait_ge(low, n * 2 + 1 + c // (K // 2))
                        pe.matmul(o, w[0][:, c, cols], zh[par][:, c, :], start=(c == 0), stop=False)
                        pe.matmul(o, w[0][:, c, cols], zl[par][:, c, :], start=False, stop=False)
                        last = pe.matmul(o, w[1][:, c, cols], zh[par][:, c, :], start=False, stop=(c == K - 1))
                    last.then_inc(product, 1)

            over_steps(pe, step)


def last_layer(nc, a, out, h_in, buf_d, stats, vec, epsln, ident, ew):
    K = CH[3] // P
    g_at, beta_at = VCOL["L0_gnn_g3"], VCOL["L0_gnn_beta3"]
    ctx = ExitStack()
    with ctx:
        def sb(name, shape, dt=F32):
            return ctx.enter_context(nc.sbuf_tensor("f_" + name, shape, dt))

        def sem(name):
            return ctx.enter_context(nc.semaphore("f_" + name))

        def two(name, shape, dt=F32):
            return [sb(f"{name}{k}", shape, dt) for k in range(2)]

        hin, zh, zl = two("hin", [P, K, GROUP]), two("zh", [P, K, GROUP], F32R), two("zl", [P, K, GROUP], F32R)
        ex = sb("ex", [P, K, GROUP])
        mv, scale, shift = sb("mv", [P, K, 2]), sb("scale", [P, K]), sb("shift", [P, K])
        xg = two("xg", [P, 4, D])
        row = [sb(f"row{k}", [P, 4, ROW]) for k in range(RING)]
        xt = sb("xt", [P, 2, GROUP])
        w4raw = xt[:, :, :].rearrange("p h (c m) -> p (h c) m", m=D)
        b4, b4h, b4l, b4z = sb("b4", [P, D]), sb("b4h", [P, D], F32R), sb("b4l", [P, D]), sb("b4z", [P, D])
        b4p = sb("b4p", [P, D], F32R)
        w4h, w4l = sb("w4h", [P, K, D], F32R), sb("w4l", [P, K, D], F32R)
        gw = sb("gw", [P, 2, NE])
        gb = sb("gb", [P, NE])
        ones, ones_r, upper = sb("ones", [P, P]), sb("ones_r", [P, P], F32R), sb("upper", [P, P])
        place = sb("place", [P, 1, NE])
        st, rmv, rs = two("st", [P, 4, 6]), two("rmv", [P, 4, 2]), two("rs", [P, 4])
        cand, onehot, hits = sb("cand", [P, 4, NE]), two("onehot", [P, 4, NE]), sb("hits", [P, 4, NE])
        best, expert, limit = sb("best", [P, 4, 1]), sb("expert", [P, 4, 1]), two("limit", [P, 4])
        slot, over = sb("slot", [P, 4]), sb("over", [P, 4])
        sidx = two("sidx", [P, 4], I32)
        here, before = sb("here", [P, NE]), two("before", [P, 1, NE])
        ps_y = [ctx.enter_context(nc.psum_tensor(f"f_ps_y{k}", [P, 4, D], F32)) for k in range(2)]
        ps_t = ctx.enter_context(nc.psum_tensor("f_ps_t", [P, 2, GROUP], F32))
        ps_l = ctx.enter_context(nc.psum_tensor("f_ps_l", [P, 4, NE], F32))
        ps_c = ctx.enter_context(nc.psum_tensor("f_ps_c", [P, 4, NE], F32))

        held, bn_done, bn_root, bn_ready = sem("held"), sem("bn_done"), sem("bn_root"), sem("bn_ready")
        small_in, const, tables, w_in, w_split = sem("small_in"), sem("const"), sem("tables"), sem("w_in"), sem("w_split")
        ew_in, ew_split = sem("ew_in"), sem("ew_split")
        loaded, x_in = [sem(f"loaded{k}") for k in range(2)], [sem(f"x_in{k}") for k in range(2)]
        exped, bounded, active, high, low = sem("exped"), sem("bounded"), sem("active"), sem("high"), sem("low")
        product, counted, moments, rooted, inverse, normed = (sem("product"), sem("counted"), sem("moments"),
                                                              sem("rooted"), sem("inverse"), sem("normed"))
        x1_kept = sem("x1_kept")
        turned, xt_kept, logits = sem("turned"), sem("xt_kept"), sem("logits")
        first, placed, second = sem("first"), sem("placed"), sem("second")
        x1_out, sent = [sem(f"x1_out{k}") for k in range(RING)], [sem(f"sent{k}") for k in range(RING)]
        ROUTE1, ROUTE2 = 8, 4
        TABLES = 5 + NE
        block = ctx.enter_context(nc.Block())

        hin_v = h_in.rearrange("(m p) n -> p m n", p=P)
        xfull = a["x"][0:LAST * GROUP, :].rearrange("(g s p) f -> g p s f", s=4, p=P)
        outfull = out[0:LAST * GROUP, :].rearrange("(g s p) f -> g p s f", s=4, p=P)

        def group(view, n):
            if static(n):
                return view[n]
            return view[bass.ds(n, 1)].rearrange("o p s f -> (o p) s f")

        def width(n):
            return TAIL if is_last(n) else GROUP

        def piped(eng, step):
            loops = (NT - 3) // RING
            for n in range(RING):
                step(n, n)
            with eng.Fori(1, loops) as i:
                for u in range(RING):
                    step(i * RING + u, u)
            for n in range(loops * RING, NT + 2):
                step(n, n % RING)

        def valid(n):
            return not static(n) or 0 <= n < NT

        def since(n, lag):
            return not static(n) or n >= lag

        def laps(n, r):
            return n // RING if static(n) else (n - r) // RING

        @block.sync
        def _(sp):
            def load_h(n, par):
                if since(n, 2):
                    sp.wait_ge(low, n - 1)
                sp.dma_start(hin[par][:, :, 0:width(n)], hin_v[:, :, bass.ds(n * GROUP, width(n))]).then_inc(loaded[par], 16)

            def load_x(n, par):
                if since(n, 2):
                    sp.wait_ge(product, n - 1)
                if not is_last(n):
                    sp.dma_start(xg[par][:, :, :], group(xfull, n)).then_inc(x_in[par], 16)
                else:
                    for s, rows in row_tiles(n):
                        at = n * GROUP + s * P
                        sp.dma_start(xg[par][0:rows, s, :], a["x"][at:at + rows, :]).then_inc(x_in[par], 16)

            def store(n, r):
                sp.wait_ge(x1_kept, n + 1)
                if not is_last(n):
                    sp.dma_start(group(outfull, n), row[r][:, :, D:2 * D]).then_inc(x1_out[r], 16)
                else:
                    for s, rows in row_tiles(n):
                        at = n * GROUP + s * P
                        sp.dma_start(out[at:at + rows, :], row[r][0:rows, s, D:2 * D]).then_inc(x1_out[r], 16)

            def step(n, r):
                if valid(n + 2):
                    load_h(n + 2, r % 2)
                    load_x(n + 2, r % 2)
                if valid(n):
                    store(n, r)

            load_h(0, 0)
            load_x(0, 0)
            load_h(1, 1)
            load_x(1, 1)
            piped(sp, step)
            for r in range(RING):
                stores = sum(len(row_tiles(n)) if is_last(n) else 1 for n in range(r, NT, RING))
                sp.wait_ge(x1_out[r], 16 * stores)

        @block.gpsimd
        def _(pool):
            pool.dma_start(b4[:, :], a["L0_gnn_b4"].rearrange("(o f) -> o f", o=1).to_broadcast([P, D])).then_inc(small_in, 16)
            pool.dma_start(gb[:, :], a["L0_ffn_gate_b"].rearrange("(o f) -> o f", o=1).to_broadcast([P, NE])).then_inc(small_in, 16)
            pool.dma_start(gw[:, :, :], a["L0_ffn_gate_w"].rearrange("(c p) e -> p c e", p=P)).then_inc(small_in, 16)
            pool.dma_start(w4raw[:, :, :], a["L0_gnn_W4"].rearrange("(c p) m -> p c m", p=P)).then_inc(w_in, 16)
            pool.dma_start(ew["w1raw"][:, :, :], a["L0_ffn_w1"][0].rearrange("(c p) m -> p c m", p=P)).then_inc(ew_in, 16)
            pool.dma_start(ew["w2raw"][:, :, :], a["L0_ffn_w2"][0].rearrange("(c p) m -> p c m", p=P)).then_inc(ew_in, 16)
            pool.dma_start(ew["b2"][0][:, 0, :], a["L0_ffn_b2"][0:1, :].to_broadcast([P, D])).then_inc(ew_in, 16)
            nc.gpsimd.memset(ones[:, :], 1.0).then_inc(const, 1)
            for e in range(NE):
                nc.gpsimd.memset(place[:, :, e:e + 1], float(e / NE)).then_inc(tables, 1)
            pool.wait_ge(w_in, 16)
            nc.gpsimd.tensor_copy(w4h[:, :, :], w4raw[:, :, :]).then_inc(w_split, 1)
            pool.wait_ge(const, 1)
            nc.gpsimd.tensor_copy(ones_r[:, :], ones[:, :]).then_inc(tables, 1)
            pool.wait_ge(w_split, 1)
            nc.gpsimd.tensor_tensor(w4l[:, :, :], w4raw[:, :, :], w4h[:, :, :].bitcast(F32), ALU.subtract).then_inc(w_split, 1)
            nc.gpsimd.affine_select(out=upper[:, :], in_=ones[:, :], compare_op=ALU.is_gt, fill=0.0,
                                    base=0, pattern=[[1, P]], channel_multiplier=-1).then_inc(tables, 1)
            for r in range(RING):
                nc.gpsimd.memset(row[r][:, :, NUMBER + 1:ROW], 0.0).then_inc(const, 1)
                nc.gpsimd.iota(row[r][:, :, NUMBER].bitcast(I32), pattern=[[P, 4]], base=(r - RING) * GROUP,
                               channel_multiplier=1).then_inc(const, 1)
            pool.wait_ge(const, 1 + 2 * RING)
            pool.sem_inc(tables, 3)
            pool.wait_ge(ew_in, 48)
            for part in ("w1", "w2"):
                nc.gpsimd.tensor_copy(ew[part + "h"][0][:, :, :], ew[part + "raw"][:, :, :]).then_inc(ew_split, 1)
            for k, part in enumerate(("w1", "w2")):
                pool.wait_ge(ew_split, k + 1)
                nc.gpsimd.tensor_tensor(ew[part + "l"][0][:, :, :], ew[part + "raw"][:, :, :],
                                        ew[part + "h"][0][:, :, :].bitcast(F32), ALU.subtract)

            def step(n, r):
                m, mr = n - 2, (r - 2) % RING
                if valid(m):
                    after(pool, second, m * ROUTE2 + ROUTE2, held)
                    for s, rows in row_tiles(m):
                        pool.indirect_dma_start(buf_d, bass.IndirectOffsetOnAxis(sidx[mr % 2][0:rows, s:s + 1], 0),
                                                row[mr][0:rows, s, :], None, bounds_check=NE * CAP - 1,
                                                oob_is_err=False).then_inc(sent[mr], 16)

            piped(pool, step)
            for r in range(RING):
                pool.wait_ge(sent[r], 16 * sum(len(row_tiles(n)) for n in range(r, NT, RING)))

        @block.scalar
        def _(act):
            act.wait_ge(bn_done, 1)
            nc.scalar.activation(scale[:, :], mv[:, :, 1], ACT.Sqrt, bias=epsln[:, 0:1]).then_inc(bn_root, 1)
            act.wait_ge(bn_ready, 3)

            def prep(n, par, half):
                w = width(n)
                if half == 0:
                    if since(n, 1):
                        act.wait_ge(active, n)
                    act.wait_ge(loaded[par], uses(n, par) * 16)
                for c in range(half * K // 2, (half + 1) * K // 2):
                    nc.scalar.activation(ex[:, c, 0:w], hin[par][:, c, 0:w], ACT.Exp, bias=shift[:, c:c + 1], scale=scale[:, c:c + 1])
                    last = nc.scalar.activation(hin[par][:, c, 0:w], hin[par][:, c, 0:w], ACT.Identity, bias=shift[:, c:c + 1],
                                                scale=scale[:, c:c + 1])
                if half == 1:
                    last.then_inc(exped, 1)

            def split(n, par):
                if since(n, 2):
                    act.wait_ge(product, n - 1)
                act.wait_ge(active, n + 1)
                nc.scalar.copy(zh[par][:, :, 0:width(n)], hin[par][:, :, 0:width(n)]).then_inc(high, 1)

            def step(n, r):
                par = r % 2
                if valid(n + 1):
                    split(n + 1, 1 - par)
                if valid(n + 2):
                    prep(n + 2, par, 0)
                if valid(n):
                    if since(n, RING):
                        act.wait_ge(sent[r], laps(n, r) * 64)
                        act.wait_ge(x1_out[r], laps(n, r) * 16)
                    act.wait_ge(product, n + 1)
                    for s0, c, rows in row_parts(n):
                        last = nc.scalar.copy(row[r][0:rows, s0:s0 + c, D:2 * D], ps_y[par][0:rows, s0:s0 + c, :])
                    last.then_inc(x1_kept, 1)
                    act.wait_ge(moments, n + 1)
                    for s0, c, rows in row_parts(n):
                        last = nc.scalar.activation(rs[par][0:rows, s0:s0 + c], rmv[par][0:rows, s0:s0 + c, 1], ACT.Sqrt,
                                                    bias=epsln[0:rows, 0:1])
                    last.then_inc(rooted, 1)
                if valid(n - 1):
                    if since(n, 2):
                        act.wait_ge(logits, n - 1)
                    act.wait_ge(turned, n)
                    nc.scalar.copy(xt[:, :, 0:width(n - 1)], ps_t[:, :, 0:width(n - 1)]).then_inc(xt_kept, 1)
                if valid(n + 2):
                    prep(n + 2, par, 1)

            for half in range(2):
                prep(0, 0, half)
            split(0, 0)
            for half in range(2):
                prep(1, 1, half)
            piped(act, step)

        @block.vector
        def _(dve):
            for c in range(K):
                last = nc.vector.bn_aggr(mv[:, c, :], stats[:, c, :, :].rearrange("p t s -> p (t s)"))
            last.then_inc(bn_done, 1)
            dve.wait_ge(bn_root, 1)
            nc.vector.reciprocal(scale[:, :], scale[:, :]).then_inc(bn_ready, 1)
            dve.wait_ge(bn_ready, 1)
            nc.vector.tensor_tensor(scale[:, :], scale[:, :], vec[:, g_at:g_at + K], ALU.mult).then_inc(bn_ready, 1)
            dve.wait_ge(bn_ready, 2)
            nc.vector.tensor_tensor(shift[:, :], scale[:, :], mv[:, :, 0], ALU.mult).then_inc(bn_done, 1)
            dve.wait_ge(bn_done, 2)
            nc.vector.tensor_tensor(shift[:, :], vec[:, beta_at:beta_at + K], shift[:, :], ALU.subtract).then_inc(bn_ready, 1)

            def prep(n, par):
                w = width(n)
                dve.wait_ge(exped, n + 1)
                nc.vector.tensor_scalar(ex[:, :, 0:w], ex[:, :, 0:w], 1.0, 0.0, ALU.subtract, ALU.min).then_inc(bounded, 1)
                dve.wait_ge(bounded, n + 1)
                nc.vector.tensor_tensor(hin[par][:, :, 0:w], hin[par][:, :, 0:w], ex[:, :, 0:w], ALU.max).then_inc(active, 1)

            def split(n, par):
                w = width(n)
                if since(n, 2):
                    dve.wait_ge(product, n - 1)
                dve.wait_ge(high, n + 1)
                nc.vector.tensor_tensor(zl[par][:, :, 0:w], hin[par][:, :, 0:w], zh[par][:, :, 0:w].bitcast(F32),
                                        ALU.subtract).then_inc(low, 1)

            def tables_once():
                dve.wait_ge(small_in, 48)
                dve.wait_ge(tables, TABLES)
                nc.vector.tensor_copy(b4h[:, :], b4[:, :]).then_inc(const, 1)
                nc.vector.tensor_scalar(gb[:, :], gb[:, :], ident[:, 0:1], None, ALU.mult).then_inc(const, 1)
                nc.vector.tensor_scalar(before[0][:, :, :], place[:, :, :], float(NE * CAP), ident[:, 0:1],
                                        ALU.mult, ALU.mult).then_inc(const, 1)
                seen = 1 + 2 * RING + 3
                dve.wait_ge(const, seen)
                nc.vector.tensor_tensor(b4l[:, :], b4[:, :], b4h[:, :].bitcast(F32), ALU.subtract).then_inc(const, 1)
                nc.vector.tensor_scalar(b4z[:, :], b4h[:, :].bitcast(F32), ident[:, 0:1], None, ALU.mult).then_inc(const, 1)
                dve.wait_ge(const, seen + 2)
                nc.vector.scalar_tensor_tensor(b4p[:, :], b4l[:, :], ident[:, 1:2], b4z[:, :], ALU.mult, ALU.add).then_inc(const, 1)

            def moments_of(n, r, par):
                after(dve, x1_kept, n + 1, held)
                for s, rows in row_tiles(n):
                    last = nc.vector.bn_stats(st[par][0:rows, s, :], row[r][0:rows, s, D:2 * D])
                last.then_inc(counted, 1)
                after(dve, counted, n + 1, held)
                for s, rows in row_tiles(n):
                    last = nc.vector.bn_aggr(rmv[par][0:rows, s, :], st[par][0:rows, s, :])
                last.then_inc(moments, 1)

            def normalise(n, r, par):
                dve.wait_ge(rooted, n + 1)
                for s0, c, rows in row_parts(n):
                    last = nc.vector.reciprocal(rs[par][0:rows, s0:s0 + c], rs[par][0:rows, s0:s0 + c])
                last.then_inc(inverse, 1)
                if since(n, RING):
                    dve.wait_ge(sent[r], laps(n, r) * 64)
                number = row[r][:, :, NUMBER].bitcast(I32)
                nc.vector.tensor_scalar(number, number, float(RING * GROUP), None, ALU.add).then_inc(inverse, 1)
                dve.wait_ge(inverse, n * 2 + 2)
                for s, rows in row_tiles(n):
                    last = nc.vector.tensor_scalar(row[r][0:rows, s, 0:D], row[r][0:rows, s, D:2 * D], rmv[par][0:rows, s, 0:1],
                                                   rs[par][0:rows, s:s + 1], ALU.subtract, ALU.mult)
                last.then_inc(normed, 1)

            def choose(n, r, par):
                def done(k):
                    dve.wait_ge(first, n * ROUTE1 + k)

                def each(op):
                    for s0, c, rows in row_parts(n):
                        last = op((slice(0, rows), slice(s0, s0 + c)), rows, c)
                    last.then_inc(first, 1)

                if is_last(n):
                    nc.vector.memset(onehot[par][:, :, :], 0.0).then_inc(const, 1)
                    dve.wait_ge(const, 1 + 2 * RING + 7)
                dve.wait_ge(logits, n + 1)
                each(lambda v, rows, c: nc.vector.tensor_reduce(best[v + (0,)], ps_l[v], AX.X, ALU.max))
                done(1)
                each(lambda v, rows, c: nc.vector.tensor_tensor(row[r][v + (slice(2 * D, NUMBER),)], ps_l[v],
                                                                best[v].to_broadcast([rows, c, NE]), ALU.subtract))
                done(2)
                each(lambda v, rows, c: nc.vector.scalar_tensor_tensor(cand[v], row[r][v + (slice(2 * D, NUMBER),)], 0.0,
                                                                       place[0:rows].to_broadcast([rows, c, NE]), ALU.is_lt, ALU.add))
                done(3)
                each(lambda v, rows, c: nc.vector.tensor_reduce(expert[v + (0,)], cand[v], AX.X, ALU.min))
                done(4)
                each(lambda v, rows, c: nc.vector.tensor_tensor(onehot[par][v], place[0:rows].to_broadcast([rows, c, NE]),
                                                                expert[v].to_broadcast([rows, c, NE]), ALU.is_equal))
                each(lambda v, rows, c: nc.vector.tensor_scalar(limit[par][v], expert[v + (0,)], float(NE * CAP), float(CAP),
                                                                ALU.mult, ALU.add))
                done(5)
                nc.vector.tensor_reduce(here[:, :], onehot[par][:, :, :].rearrange("p s e -> p e s"), AX.X, ALU.add).then_inc(first, 1)
                done(7)
                nc.vector.tensor_tensor(before[1 - par][:, 0, :], before[par][:, 0, :], here[:, :], ALU.add).then_inc(first, 1)

            def assign(n, r, par):
                def done(k):
                    dve.wait_ge(second, n * ROUTE2 + k)

                def each(op):
                    for s0, c, rows in row_parts(n):
                        last = op((slice(0, rows), slice(s0, s0 + c)))
                    last.then_inc(second, 1)

                if since(n, 1):
                    done(0)
                dve.wait_ge(placed, n + 1)
                each(lambda v: nc.vector.tensor_tensor(hits[v], ps_c[v], onehot[par][v], ALU.mult))
                done(1)
                each(lambda v: nc.vector.tensor_reduce(slot[v], hits[v], AX.X, ALU.add))
                done(2)
                each(lambda v: nc.vector.tensor_tensor(over[v], slot[v], limit[par][v], ALU.is_ge))
                done(3)
                if since(n, 2):
                    m, mr = n - 2, (r - 2) % RING
                    dve.wait_ge(sent[mr], (laps(m, mr) + 1) * 64)
                each(lambda v: nc.vector.scalar_tensor_tensor(sidx[par][v], over[v], float(FAR), slot[v], ALU.mult, ALU.add))

            def step(n, r):
                par = r % 2
                if valid(n + 1):
                    prep(n + 1, 1 - par)
                    split(n + 1, 1 - par)
                if static(n) and n == 0:
                    tables_once()
                if valid(n):
                    moments_of(n, r, par)
                if valid(n - 2):
                    assign(n - 2, (r - 2) % RING, par)
                if valid(n):
                    normalise(n, r, par)
                if valid(n - 1):
                    choose(n - 1, (r - 1) % RING, 1 - par)

            prep(0, 0)
            split(0, 0)
            piped(dve, step)

        @block.tensor
        def _(pe):
            pe.wait_ge(w_split, 2)
            pe.wait_ge(const, 1 + 2 * RING + 6)

            def rows_of(n, par):
                pe.wait_ge(low, n + 1)
                pe.wait_ge(x_in[par], (uses(n, par) - 1 + (len(row_tiles(n)) if is_last(n) else 1)) * 16)
                if since(n, 2):
                    pe.wait_ge(x1_kept, n - 1)
                for s, rows in row_tiles(n):
                    o = ps_y[par][0:rows, s, :]
                    cols = slice(s * P, s * P + rows)
                    pe.matmul(o, ident[0:rows, 0:rows], xg[par][0:rows, s, :], start=True, stop=False)
                    pe.matmul(o, ones_r[:, 0:rows], b4p[:, :], start=False, stop=False)
                    for c in range(K):
                        pe.matmul(o, zh[par][:, c, cols], w4h[:, c, :], start=False, stop=False)
                        pe.matmul(o, zh[par][:, c, cols], w4l[:, c, :], start=False, stop=False)
                        last = pe.matmul(o, zl[par][:, c, cols], w4h[:, c, :], start=False, stop=(c == K - 1))
                last.then_inc(product, 1)

            def turn(n, r):
                if since(n, 1):
                    pe.wait_ge(xt_kept, n)
                pe.wait_ge(normed, n + 1)
                for h in range(2):
                    for s, rows in row_tiles(n):
                        last = pe.transpose(ps_t[:, h, s * P:s * P + rows], row[r][0:rows, s, h * P:(h + 1) * P], ident[0:rows, 0:rows])
                last.then_inc(turned, 1)

            def score(n):
                if since(n, 1):
                    pe.wait_ge(first, n * ROUTE1 - ROUTE1 + 2)
                pe.wait_ge(xt_kept, n + 1)
                for s, rows in row_tiles(n):
                    pe.matmul(ps_l[0:rows, s, :], ones[:, 0:rows], gb[:, :], start=True, stop=False)
                    for h in range(2):
                        last = pe.matmul(ps_l[0:rows, s, :], xt[:, h, s * P:s * P + rows], gw[:, h, :], start=False, stop=(h == 1))
                last.then_inc(logits, 1)

            def count(n, par):
                if since(n, 1):
                    pe.wait_ge(second, n * ROUTE2 - ROUTE2 + 1)
                pe.wait_ge(first, n * ROUTE1 + ROUTE1)
                pe.matmul(ps_c[:, :, :], ones[:, :], before[par][:, :, :].to_broadcast([P, 4, NE]), start=True, stop=False)
                for t in range(3):
                    pe.matmul(ps_c[:, t + 1:4, :], ones[:, :], onehot[par][:, t:t + 1, :].to_broadcast([P, 3 - t, NE]),
                              start=False, stop=False)
                pe.matmul(ps_c[:, :, :], upper[:, :], onehot[par][:, :, :], start=False, stop=True).then_inc(placed, 1)

            def step(n, r):
                if valid(n):
                    rows_of(n, r % 2)
                if valid(n - 1):
                    turn(n - 1, (r - 1) % RING)
                if valid(n - 2):
                    count(n - 2, r % 2)
                if valid(n - 1):
                    score(n - 1)

            piped(pe, step)


def experts(nc, a, buf_d, out, ident, b1e, ew):
    ctx = ExitStack()
    with ctx:
        def sb(name, shape, dt=F32):
            return ctx.enter_context(nc.sbuf_tensor("g_" + name, shape, dt))

        def sem(name):
            return ctx.enter_context(nc.semaphore("g_" + name))

        def two(name, shape, dt=F32):
            return [sb(f"{name}{k}", shape, dt) for k in range(2)]

        FC, DC, TPE = F // P, D // P, len(XT)
        w1h, w1l, w2h, w2l, b2 = ew["w1h"], ew["w1l"], ew["w2h"], ew["w2l"], ew["b2"]
        xin = [sb(f"xin{k}", [P, 4, ROW]) for k in range(TPE)]
        xh, xl = two("xh", [P, DC, GROUP], F32R), two("xl", [P, DC, GROUP], F32R)
        HID = 4
        hid = sb("hid", [P, HID, GROUP])
        hh, hl = sb("hh", [P, FC, GROUP], F32R), sb("hl", [P, FC, GROUP], F32R)
        expd, total, prob = sb("expd", [P, 4, NE]), sb("total", [P, 4]), two("prob", [P, 4])
        ysb, odd, above, below = two("ysb", [P, 4, D]), sb("odd", [P, 4, D]), sb("above", [P, 4, D]), sb("below", [P, 4, D])
        ps_t = ctx.enter_context(nc.psum_tensor("g_ps_t", [P, DC, GROUP], F32))
        ps_h = [ctx.enter_context(nc.psum_tensor(f"g_ps_h{k}", [P, GROUP], F32)) for k in range(4)]
        ps_y = ctx.enter_context(nc.psum_tensor("g_ps_y", [P, 4, D], F32))

        held = sem("held")
        w_in, w_high, w_split = sem("w_in"), sem("w_high"), sem("w_split")
        x_in, y_out = [sem(f"x_in{k}") for k in range(TPE)], [sem(f"y_out{k}") for k in range(TPE)]
        turned, x_high, x_low, up, hidden, hid_low, down = (sem("turned"), sem("x_high"), sem("x_low"), sem("up"),
                                                            sem("hidden"), sem("hid_low"), sem("down"))
        expl, summed, gate = sem("expl"), sem("summed"), sem("gate")
        emptied, gated, parted, joined, cleaned, y_ready = (sem("emptied"), sem("gated"), sem("parted"), sem("joined"),
                                                            sem("cleaned"), sem("y_ready"))
        block = ctx.enter_context(nc.Block())

        def tiles(q):
            return [(s, min(P, XT[q] - s * P)) for s in range(-(-XT[q] // P))]

        def over_tiles(eng, tile):
            def body(i):
                for u in range(2 * TPE):
                    tile(i * (2 * TPE) + u, i * 2 + u // TPE, u // TPE, u % TPE)

            body(0)
            with eng.Fori(1, NE // 2) as i:
                body(i)

        def since(t, lag):
            return not static(t) or t >= lag

        @block.sync
        def _(sp):
            def load(e, q):
                if since(e, 1):
                    sp.wait_ge(y_out[q], e * (16 * len(tiles(q))))
                sp.dma_start(xin[q][:, :, :], buf_d[bass.ds(e * CAP + q * GROUP, GROUP), :].rearrange("(s p) f -> p s f", p=P)
                             ).then_inc(x_in[q], 16)

            def weights(e, k):
                if since(e, 1):
                    after(sp, w_split, e, held)
                    after(sp, emptied, e * TPE, held)
                n = (e + 1) % NE
                o = "o p c m -> p (o c) m"
                sp.dma_start(ew["w1raw"][:, :, :], a["L0_ffn_w1"][bass.ds(n, 1)].rearrange("o (c p) m -> o p c m", p=P).rearrange(o)).then_inc(w_in, 16)
                sp.dma_start(ew["w2raw"][:, :, :], a["L0_ffn_w2"][bass.ds(n, 1)].rearrange("o (c p) m -> o p c m", p=P).rearrange(o)).then_inc(w_in, 16)
                sp.dma_start(b2[1 - k][:, 0, :], a["L0_ffn_b2"][bass.ds(n, 1), :].to_broadcast([P, D])).then_inc(w_in, 16)

            def tile(t, e, k, q):
                if q == 0:
                    weights(e, k)
                load(e + (q + 2) // TPE, (q + 2) % TPE)

            load(0, 0)
            load(0, 1)
            over_tiles(sp, tile)
            for q in range(2):
                sp.wait_ge(x_in[q], 16 * (NE + 1))
            sp.wait_ge(w_in, 48 * NE)

        @block.gpsimd
        def _(pool):
            def tile(t, e, k, q):
                after(pool, y_ready, t + 1, held)
                for s, rows in tiles(q):
                    pool.indirect_dma_start(out, bass.IndirectOffsetOnAxis(xin[q][0:rows, s, NUMBER:NUMBER + 1].bitcast(I32), 0),
                                            ysb[q % 2][0:rows, s, :], None, bounds_check=N - 1, oob_is_err=False
                                            ).then_inc(y_out[q], 16)

            over_tiles(pool, tile)
            for q in range(TPE):
                pool.wait_ge(y_out[q], NE * 16 * len(tiles(q)))

        @block.scalar
        def _(act):
            def high(t, e, q):
                act.wait_ge(turned, t + 1)
                nc.scalar.copy(xh[q % 2][:, :, 0:XT[q]], ps_t[:, :, 0:XT[q]]).then_inc(x_high, 1)
                act.wait_ge(x_in[q], e * 16 + 16)
                if since(t, 1):
                    act.wait_ge(summed, t)
                nc.scalar.activation(expd[:, :, :], xin[q][:, :, 2 * D:NUMBER], ACT.Exp).then_inc(expl, 1)

            def tile(t, e, k, q):
                for f in range(FC):
                    b = b1e[:, bass.ds(e * FC + f, 1)]
                    if since(t, 1) or f >= HID:
                        act.wait_ge(hid_low, t * FC + (f + 1 - HID))
                    after(act, up, t * FC + f + 1, held)
                    if f == 0 and since(t, 1):
                        after(act, down, t, held)
                    nc.scalar.activation(hid[:, f % HID, 0:XT[q]], ps_h[f % 4][:, 0:XT[q]], ACT.Relu, bias=b)
                    nc.scalar.activation(hh[:, f, 0:XT[q]], ps_h[f % 4][:, 0:XT[q]], ACT.Relu, bias=b).then_inc(hidden, 1)
                high(t + 1, e + (q + 1) // TPE, (q + 1) % TPE)
                if q == 1:
                    act.wait_ge(w_in, e * 48 + 48)
                    nc.scalar.copy(w1h[1 - k][:, :, :], ew["w1raw"][:, :, :])
                    nc.scalar.copy(w2h[1 - k][:, :, :], ew["w2raw"][:, :, :]).then_inc(w_high, 1)

            high(0, 0, 0)
            over_tiles(act, tile)

        @block.vector
        def _(dve):
            def rest(t, q):
                dve.wait_ge(x_high, t + 1)
                nc.vector.tensor_tensor(xl[q % 2][:, :, 0:XT[q]], ps_t[:, :, 0:XT[q]], xh[q % 2][:, :, 0:XT[q]].bitcast(F32),
                                        ALU.subtract).then_inc(x_low, 1)
                dve.wait_ge(expl, t + 1)
                nc.vector.tensor_reduce(total[:, :], expd[:, :, :], AX.X, ALU.add).then_inc(summed, 1)
                dve.wait_ge(summed, t + 1)
                nc.vector.reciprocal(prob[q % 2][:, :], total[:, :]).then_inc(gate, 1)

            def finish(t, e, k, q):
                y = ysb[q % 2]

                def bias():
                    if since(t, 2):
                        last = (q - 2) % TPE
                        dve.wait_ge(y_out[last], (e - (0 if q >= 2 else 1) + 1) * (16 * len(tiles(last))))
                    dve.wait_ge(down, t + 1)
                    nc.vector.tensor_tensor(y[:, :, :], ps_y[:, :, :], b2[k][:, :, :].to_broadcast([P, 4, D]), ALU.add).then_inc(emptied, 1)

                def times_gate():
                    dve.wait_ge(gate, t + 1)
                    dve.wait_ge(emptied, t + 1)
                    for s in range(4):
                        last = nc.vector.tensor_scalar(y[:, s, :], y[:, s, :], prob[q % 2][:, s:s + 1], None, ALU.mult)
                    last.then_inc(gated, 1)

                def part():
                    dve.wait_ge(gated, t + 1)
                    nc.vector.tensor_scalar(odd[:, :, :], y[:, :, :], 0.0, 0.0, ALU.mult, ALU.not_equal)
                    nc.vector.tensor_scalar(above[:, :, :], y[:, :, :], 0.0, 1e4, ALU.max, ALU.min)
                    nc.vector.tensor_scalar(below[:, :, :], y[:, :, :], 0.0, -1e4, ALU.min, ALU.max).then_inc(parted, 1)

                def join():
                    dve.wait_ge(parted, t + 1)
                    nc.vector.tensor_tensor(above[:, :, :], above[:, :, :], below[:, :, :], ALU.add).then_inc(joined, 1)

                def clean():
                    after(dve, joined, t + 1, held)
                    nc.vector.copy_predicated(y[:, :, :], odd[:, :, :].bitcast(I32), above[:, :, :]).then_inc(cleaned, 1)

                def add():
                    dve.wait_ge(cleaned, t + 1)
                    nc.vector.tensor_tensor(y[:, :, :], y[:, :, :], xin[q][:, :, D:2 * D], ALU.add).then_inc(y_ready, 1)

                return [bias, times_gate, part, join, clean, add]

            def tile(t, e, k, q):
                steps = []
                if since(t, 1):
                    steps = finish(t - 1, e - (0 if q else 1), k if q else 1 - k, (q - 1) % TPE)
                for f in range(FC):
                    if f < len(steps):
                        steps[f]()
                    dve.wait_ge(hidden, t * FC + f + 1)
                    nc.vector.tensor_tensor(hl[:, f, 0:XT[q]], hid[:, f % HID, 0:XT[q]], hh[:, f, 0:XT[q]].bitcast(F32),
                                            ALU.subtract).then_inc(hid_low, 1)
                rest(t + 1, (q + 1) % TPE)
                if q == 2:
                    dve.wait_ge(w_high, e + 1)
                    nc.vector.tensor_tensor(w1l[1 - k][:, :, :], ew["w1raw"][:, :, :], w1h[1 - k][:, :, :].bitcast(F32), ALU.subtract)
                    nc.vector.tensor_tensor(w2l[1 - k][:, :, :], ew["w2raw"][:, :, :], w2h[1 - k][:, :, :].bitcast(F32),
                                            ALU.subtract).then_inc(w_split, 1)

            rest(0, 0)
            over_tiles(dve, tile)
            for do in finish(NE * TPE - 1, NE - 1, 1, TPE - 1):
                do()

        @block.tensor
        def _(pe):
            def turn(t, e, q):
                pe.wait_ge(x_in[q], e * 16 + 16)
                if since(t, 1):
                    pe.wait_ge(x_low, t)
                for h in range(DC):
                    for s in range(4):
                        last = pe.transpose(ps_t[:, h, s * P:(s + 1) * P], xin[q][:, s, h * P:(h + 1) * P], ident[:, :])
                last.then_inc(turned, 1)

            def tile(t, e, k, q):
                if q == 0 and since(e, 1):
                    pe.wait_ge(w_split, e)
                pe.wait_ge(x_low, t + 1)
                for f in range(FC):
                    if since(t, 1) or f >= 4:
                        pe.wait_ge(hidden, t * FC + (f + 1 - 4))
                    o = ps_h[f % 4][:, 0:XT[q]]
                    cols = slice(f * P, (f + 1) * P)
                    for c in range(DC):
                        pe.matmul(o, w1h[k][:, c, cols], xh[q % 2][:, c, 0:XT[q]], start=(c == 0), stop=False)
                        pe.matmul(o, w1h[k][:, c, cols], xl[q % 2][:, c, 0:XT[q]], start=False, stop=False)
                        last = pe.matmul(o, w1l[k][:, c, cols], xh[q % 2][:, c, 0:XT[q]], start=False, stop=(c == DC - 1))
                    last.then_inc(up, 1)
                turn(t + 1, e + (q + 1) // TPE, (q + 1) % TPE)
                if since(t, 1):
                    pe.wait_ge(emptied, t)
                for s in range(4):
                    o = ps_y[:, s, :]
                    cols = slice(s * P, (s + 1) * P)
                    for f in range(FC):
                        if s == 0:
                            pe.wait_ge(hid_low, t * FC + f + 1)
                        pe.matmul(o, hh[:, f, cols], w2h[k][:, f, :], start=(f == 0), stop=False)
                        pe.matmul(o, hh[:, f, cols], w2l[k][:, f, :], start=False, stop=False)
                        last = pe.matmul(o, hl[:, f, cols], w2h[k][:, f, :], start=False, stop=(f == FC - 1))
                last.then_inc(down, 1)

            turn(0, 0, 0)
            over_tiles(pe, tile)


_INS = ["x", "src", "dst", "L0_gnn_eps", "L0_gnn_W1", "L0_gnn_b1", "L0_gnn_g1", "L0_gnn_beta1", "L0_gnn_W2", "L0_gnn_b2",
        "L0_gnn_g2", "L0_gnn_beta2", "L0_gnn_W3", "L0_gnn_b3", "L0_gnn_g3", "L0_gnn_beta3", "L0_gnn_W4", "L0_gnn_b4",
        "L0_ffn_gate_w", "L0_ffn_gate_b", "L0_ffn_w1", "L0_ffn_b1", "L0_ffn_w2", "L0_ffn_b2"]


def kernel(**inputs):
    import numpy as np
    import concourse.bacc as bacc
    from concourse import mybir as mb
    from concourse.bass_utils import run_bass_kernel_spmd

    nc = bacc.Bacc("TRN2", target_bir_lowering=False, num_devices=1)
    arrays, args = {}, {}
    for name in _INS:
        v = np.ascontiguousarray(inputs[name])
        arrays[f"in_{name}_dram"] = v
        args[name] = nc.dram_tensor(f"in_{name}_dram", v.shape, mb.dt.from_np(v.dtype), kind="ExternalInput").ap()
    out = nc.dram_tensor("out_0_dram", (N, D), mb.dt.float32, kind="ExternalOutput").ap()
    gnn_ffn_program(nc, args, out)
    r = run_bass_kernel_spmd(nc, [arrays], core_ids=[0])
    return r.results[0]["out_0_dram"]
```
